# Optimizing a Trainium2 kernel written in Bass

```python
import numpy as np
import jax
import jax.numpy as jnp

def _softmax(x, axis=-1):
    return jax.nn.softmax(x, axis=axis)

def _gelu(x):
    return jax.nn.gelu(x, approximate=True)

def _silu(x):
    return jax.nn.silu(x)

def _sigmoid(x):
    return jax.nn.sigmoid(x)

def _layernorm(x, axis=-1, eps=1e-05):
    m = jnp.mean(x, axis=axis, keepdims=True)
    v = jnp.var(x, axis=axis, keepdims=True)
    return (x - m) / jnp.sqrt(v + eps)

def _scatter_add(tgt, idx, src, axis=0):
    return tgt.at[idx].add(src)

def _segment_sum(src, seg, n):
    return jax.ops.segment_sum(src, seg, n)
kernel_name = 'mk_adaln_ffn_d2_seqx_r8_b7771c'

def setup_inputs(seed: int=0):
    np.random.seed(seed)
    _w = jnp.asarray

    def _rec_inputs():
        import jax
        import jax.numpy as jnp
        _rk = jax.random.key(seed)
        x = -0.000125 + 0.9999 * jax.random.normal(jax.random.fold_in(_rk, 1), (64, 32, 256), jnp.float32)
        _lenS = 32 - jax.random.randint(jax.random.fold_in(_rk, 7), (64,), 0, max(1, 32 // 4) + 1, jnp.int32)
        _lenS2 = 32 - jax.random.randint(jax.random.fold_in(_rk, 8), (64,), 0, max(1, 32 // 4) + 1, jnp.int32)
        itok_B_0_7 = jax.random.randint(jax.random.fold_in(_rk, 11), (64,), 0, 8, jnp.int32)
        fside_8xS_0 = -0.00162727 + 0.0609077 * jax.random.normal(jax.random.fold_in(_rk, 12), (8, 32), jnp.float32)
        itok_B_0_15 = jax.random.randint(jax.random.fold_in(_rk, 13), (64,), 0, 16, jnp.int32)
        return (x, itok_B_0_7, fside_8xS_0, itok_B_0_15)
    x, itok_B_0_7, fside_8xS_0, itok_B_0_15 = _rec_inputs()

    def _L0_cond_setup():
        import jax, jax.numpy as jnp
        import numpy as np
        B, C, T = (64, 32, 256)
        D, N = (32, 8)
        key = jax.random.key(seed)
        k_x, k_s, k_w, k_b = jax.random.split(key, 4)
        scale = 1.0 / np.sqrt(C)
        x = jax.random.normal(k_x, (B, C, T), dtype=jnp.float32)
        subjects = jax.random.randint(k_s, (B,), 0, N, dtype=jnp.int64)
        weights = jax.random.normal(k_w, (N, C, D), dtype=jnp.float32) * scale
        bias = jax.random.normal(k_b, (N, D), dtype=jnp.float32) * scale
        return {'x': x, 'subjects': subjects, 'weights': weights, 'bias': bias}
    _L0_cond_all = _L0_cond_setup()
    _L0_cond_in = {k: v for k, v in _L0_cond_all.items() if k in ('weights',)}
    del _L0_cond_all

    def _L0_ffn_setup():
        import jax, jax.numpy as jnp
        import numpy as np
        B, S, D, K, R = (4, 256, 256, 8, 64)
        key = jax.random.key(seed)
        ks = jax.random.split(key, 7)
        x = jax.random.normal(ks[0], (B, S, D), dtype=jnp.float32)
        U = jax.random.normal(ks[1], (K, D, R), dtype=jnp.float32) * 0.02
        V = jax.random.normal(ks[2], (K, R, D), dtype=jnp.float32) * 0.02
        W1 = jax.random.normal(ks[3], (D, D), dtype=jnp.float32) * 0.02
        b1 = jnp.zeros((D,), dtype=jnp.float32)
        W2 = jax.random.normal(ks[4], (D, K), dtype=jnp.float32) * 0.02
        b2 = jnp.zeros((K,), dtype=jnp.float32)
        return {'x': x, 'U': U, 'V': V, 'W1': W1, 'b1': b1, 'W2': W2, 'b2': b2}
    _L0_ffn_all = _L0_ffn_setup()
    _L0_ffn_in = {k: v for k, v in _L0_ffn_all.items() if k in ('U', 'V', 'W1', 'b1', 'W2', 'b2')}
    del _L0_ffn_all

    def _L1_cond_setup():
        import jax, jax.numpy as jnp
        import numpy as np
        key = jax.random.key(seed)
        k1, k2, k3, k4 = jax.random.split(key, 4)
        B, S, IN, OUT, E = (64, 32, 256, 256, 16)
        bound = 1.0 / np.sqrt(IN)
        x = jax.random.normal(k1, (B, S, IN), dtype=jnp.float32)
        idx = jax.random.randint(k2, (B,), 0, E, dtype=jnp.int64)
        W = jax.random.uniform(k3, (E, IN, OUT), dtype=jnp.float32, minval=-bound, maxval=bound)
        b = jnp.full((E, OUT), 0.1, dtype=jnp.float32)
        return {'x': x, 'id': idx, 'W': W, 'b': b}
    _L1_cond_all = _L1_cond_setup()
    _L1_cond_in = {k: v for k, v in _L1_cond_all.items() if k in ('W', 'b')}
    del _L1_cond_all

    def _L1_ffn_setup():
        import jax, jax.numpy as jnp
        import numpy as np
        TOP_K = 6
        CAP_FACTOR = 2

        def _shared_swiglu(x, wg, wu, wd):
            return jax.nn.silu(x @ wg.T) * (x @ wu.T) @ wd.T
        key = jax.random.key(seed)
        ks = jax.random.split(key, 8)
        B, S, D, E, F, FS = (4, 256, 256, 64, 176, 352)
        scale = jnp.float32(0.02)
        return {'hidden_states': jax.random.normal(ks[0], (B, S, D), jnp.float32), 'gate_w': jax.random.normal(ks[1], (E, D), jnp.float32) * scale, 'w_gate': jax.random.normal(ks[2], (E, F, D), jnp.float32) * scale, 'w_up': jax.random.normal(ks[3], (E, F, D), jnp.float32) * scale, 'w_down': jax.random.normal(ks[4], (E, D, F), jnp.float32) * scale, 'sh_gate': jax.random.normal(ks[5], (FS, D), jnp.float32) * scale, 'sh_up': jax.random.normal(ks[6], (FS, D), jnp.float32) * scale, 'sh_down': jax.random.normal(ks[7], (D, FS), jnp.float32) * scale}
    _L1_ffn_all = _L1_ffn_setup()
    _L1_ffn_in = {k: v for k, v in _L1_ffn_all.items() if k in ('gate_w', 'w_gate', 'w_up', 'w_down', 'sh_gate', 'sh_up', 'sh_down')}
    del _L1_ffn_all
    return {'x': x, 'itok_B_0_7': itok_B_0_7, 'fside_8xS_0': fside_8xS_0, 'itok_B_0_15': itok_B_0_15, 'L0_cond_weights': _L0_cond_in['weights'], 'L0_ffn_U': _L0_ffn_in['U'], 'L0_ffn_V': _L0_ffn_in['V'], 'L0_ffn_W1': _L0_ffn_in['W1'], 'L0_ffn_b1': _L0_ffn_in['b1'], 'L0_ffn_W2': _L0_ffn_in['W2'], 'L0_ffn_b2': _L0_ffn_in['b2'], 'L1_cond_W': _L1_cond_in['W'], 'L1_cond_b': _L1_cond_in['b'], 'L1_ffn_gate_w': _L1_ffn_in['gate_w'], 'L1_ffn_w_gate': _L1_ffn_in['w_gate'], 'L1_ffn_w_up': _L1_ffn_in['w_up'], 'L1_ffn_w_down': _L1_ffn_in['w_down'], 'L1_ffn_sh_gate': _L1_ffn_in['sh_gate'], 'L1_ffn_sh_up': _L1_ffn_in['sh_up'], 'L1_ffn_sh_down': _L1_ffn_in['sh_down']}

def reference(x, itok_B_0_7, fside_8xS_0, itok_B_0_15, L0_cond_weights, L0_ffn_U, L0_ffn_V, L0_ffn_W1, L0_ffn_b1, L0_ffn_W2, L0_ffn_b2, L1_cond_W, L1_cond_b, L1_ffn_gate_w, L1_ffn_w_gate, L1_ffn_w_up, L1_ffn_w_down, L1_ffn_sh_gate, L1_ffn_sh_up, L1_ffn_sh_down):
    import jax
    import jax.numpy as jnp

    def _L0_cond_ref(x, subjects, weights, bias):
        import jax, jax.numpy as jnp
        import numpy as np
        B, C, T = (64, 32, 256)
        D, N = (32, 8)
        w = weights[subjects]
        b = bias[subjects]
        out = jnp.einsum('bct,bcd->bdt', x, w)
        out = out + b[:, :, None]
        return out

    def _L0_ffn_ref(x, U, V, W1, b1, W2, b2):
        import jax, jax.numpy as jnp
        import numpy as np
        B, S, D, K, R = (4, 256, 256, 8, 64)
        h = jax.nn.relu(jnp.einsum('bsd,de->bse', x, W1) + b1)
        alpha = jax.nn.softmax(jnp.einsum('bse,ek->bsk', h, W2) + b2, axis=-1)
        vx = jnp.einsum('krd,bsd->bskr', V, x)
        uvx = jnp.einsum('kdr,bskr->bskd', U, vx)
        out = jnp.einsum('bsk,bskd->bsd', alpha, uvx)
        return out

    def _L1_cond_ref(x, id, W, b):
        import jax, jax.numpy as jnp
        import numpy as np
        Wg = W[id]
        bg = b[id]
        out = jnp.einsum('bsi,bio->bso', x, Wg) + bg[:, None, :]
        return out

    def _L1_ffn_ref(hidden_states, gate_w, w_gate, w_up, w_down, sh_gate, sh_up, sh_down):
        import jax, jax.numpy as jnp
        import numpy as np
        TOP_K = 6
        CAP_FACTOR = 2

        def _shared_swiglu(x, wg, wu, wd):
            return jax.nn.silu(x @ wg.T) * (x @ wu.T) @ wd.T
        B, S, D = hidden_states.shape
        E = gate_w.shape[0]
        x = hidden_states.reshape(-1, D)
        N = x.shape[0]
        A = N * TOP_K
        C = CAP_FACTOR * ((A + E - 1) // E)
        scores = jax.nn.softmax(x @ gate_w.T, axis=-1)
        topk_w, topk_idx = jax.lax.top_k(scores, TOP_K)
        topk_w = topk_w / (topk_w.sum(-1, keepdims=True) + 1e-20)
        flat_e = topk_idx.reshape(-1)
        flat_w = topk_w.reshape(-1)
        order = jnp.argsort(flat_e)
        se = flat_e[order]
        st = order // TOP_K
        sw = flat_w[order]
        counts = jnp.bincount(flat_e, length=E)
        offsets = jnp.cumsum(counts) - counts
        pos = jnp.arange(A) - offsets[se]
        valid = pos < C
        pos_c = jnp.minimum(pos, C - 1)
        buf = jnp.zeros((E, C, D), x.dtype).at[se, pos_c].add(jnp.where(valid[:, None], x[st], jnp.zeros((), x.dtype)))
        g = jnp.einsum('ecd,efd->ecf', buf, w_gate)
        u = jnp.einsum('ecd,efd->ecf', buf, w_up)
        eo = jnp.einsum('ecf,edf->ecd', jax.nn.silu(g) * u, w_down)
        gathered = eo[se, pos_c] * (sw * valid.astype(sw.dtype))[:, None]
        y = jnp.zeros_like(x).at[st].add(gathered).reshape(B, S, D)
        return y + _shared_swiglu(hidden_states, sh_gate, sh_up, sh_down)
    x = x + _L0_ffn_ref(_L0_cond_ref(x, itok_B_0_7, L0_cond_weights, fside_8xS_0), L0_ffn_U, L0_ffn_V, L0_ffn_W1, L0_ffn_b1, L0_ffn_W2, L0_ffn_b2)
    x = x + _L1_ffn_ref(_L1_cond_ref(x, itok_B_0_15, L1_cond_W, L1_cond_b), L1_ffn_gate_w, L1_ffn_w_gate, L1_ffn_w_up, L1_ffn_w_down, L1_ffn_sh_gate, L1_ffn_sh_up, L1_ffn_sh_down)
    return x

_drawn_inputs = setup_inputs


def setup_inputs(seed=0):
    import zlib

    import numpy as np

    out = dict(_drawn_inputs(seed))
    spreads = {'L0_ffn_b1': (0.0, 0.1), 'L0_ffn_b2': (0.0, 0.1), 'L1_cond_b': (0.10000000149011612, 0.2)}
    factors = {}
    for name, (base, spread) in spreads.items():
        noise = np.random.default_rng([zlib.crc32(name.encode()), seed]).standard_normal(out[name].shape)
        drawn = base * np.exp(spread * noise) if base else spread * noise
        out[name] = jnp.asarray(drawn.astype(out[name].dtype))
    for name, factor in factors.items():
        out[name] = (out[name] * factor).astype(out[name].dtype)
    return out
```

```python
from contextlib import ExitStack

import concourse.bass as bass
from concourse import mybir

F32 = mybir.dt.float32
BF16 = mybir.dt.bfloat16
I32 = mybir.dt.int32
U32 = mybir.dt.uint32
ALU = mybir.AluOpType
ACT = mybir.ActivationFunctionType
AX = mybir.AxisListType

P = 128
B, S, D = 64, 32, 256
N = B * S
NS0, NS1 = 8, 16
K0, R0 = 8, 64
E, TOPK, F, FS = 64, 6, 176, 352
CAP = 2 * ((N * TOPK + E - 1) // E)
DC = D // P
G = 4
GT = N // G
TG = GT // P
TT = N // P
BG = B // G
BT = P // S
KR = K0 * R0
KC = KR // P
TJ = CAP // P
LROWS = P * E * TJ
FR, FT = P, F - P
CU = 64
WROW = DC * (FR + CU + FT + FR) + D
SCH = [(0, P), (P, P), (2 * P, FS - 2 * P)]
NW = 8
UE = 4
assert TJ * P == CAP and G * GT == N and BG % NW == 0


def program(nc, x, xT, idq0, idb0, idb1, w0, fs0, W1, b1, W2, b2, VT, UT, cW, cb, gT, wblk, wdt, sgu, sd, out):
    ctx = ExitStack()
    with ctx:
        def sb(name, shape, dt=F32):
            return ctx.enter_context(nc.sbuf_tensor(name, shape, dt))

        def sem(name):
            return ctx.enter_context(nc.semaphore(name))

        rows = nc.dram_tensor("token_rows", [N + P, D], F32).ap()
        table = nc.dram_tensor("slot_table", [LROWS, 2], I32).ap()
        acc = [nc.dram_tensor(f"acc{j}", [N + P, D], F32).ap() for j in range(TJ)]

        ident = sb("ident", [P, P])
        identb = sb("identb", [P, P], BF16)
        tri = sb("tri", [P, P], BF16)
        onesb = sb("onesb", [P, P], BF16)
        ones8 = sb("ones8", [NS0, P])
        sel = sb("sel", [3 * K0, KR], BF16)
        iota64 = sb("iota64", [P, E])
        e_off = sb("e_off", [P, E])
        pcol = sb("pcol", [P, 1])
        iota_i = sb("iota_i", [P, E], I32)
        e_off_i = sb("e_off_i", [P, E], I32)
        pcol_i = sb("pcol_i", [P, 1], I32)
        tokid = sb("tokid", [P, TT], I32)
        zrow = sb("zrow", [P, D])
        linit = sb("linit", [P, E * TJ, 2], I32)
        i_q0 = sb("i_q0", [P, TT], I32)
        f_q0 = sb("f_q0", [P, TT])
        i_b0 = sb("i_b0", [NS0, B], I32)
        i_b1 = sb("i_b1", [NS1, B], I32)
        f_b0 = sb("f_b0", [NS0, B])
        f_b1 = sb("f_b1", [NS1, B])
        oh1 = sb("oh1", [NS1, B])
        wall = sb("wall", [P, NS0, S])
        maskq = sb("maskq", [P, NS0, TT], U32)
        gath0 = sb("gath0", [P, TT, S])
        bd = sb("bd", [P, TT, P])
        fs_s = sb("fs_s", [NS0, S])
        bias0 = sb("bias0", [NS0, B, S])
        W1s = sb("W1s", [P, DC, D])
        b1s = sb("b1s", [P, DC])
        W2s = sb("W2s", [P, DC, K0])
        b2s = sb("b2s", [P, K0])
        VTs = sb("VTs", [P, DC, KR])
        UTs = sb("UTs", [P, KC, D])
        cbs = sb("cbs", [NS1, D])
        cbT = sb("cbT", [P, DC, B])
        gTs = sb("gTs", [P, DC, E])
        sgus = sb("sgus", [P, DC, 2, FS])
        sds = sb("sds", [P, len(SCH), D])
        base = sb("base", [P, TT, D])
        cT_all = sb("cT_all", [P, DC, N])
        x_g = sb("x_g", [P, TG, D])
        xT_g = sb("xT_g", [P, DC, GT])
        h0T = sb("h0T", [P, DC, GT])
        hT = sb("hT", [P, DC, GT])
        lg = sb("lg", [P, TG, K0])
        lgm = sb("lgm", [P, TG])
        alp = sb("alp", [P, TG, K0])
        alr = sb("alr", [P, TG, K0])
        als = sb("als", [P, TG, K0, 3], BF16)
        alT = sb("alT", [3 * K0, GT], BF16)
        spread = sb("spread", [P, 2, GT])
        z = sb("z", [P, KC, GT])
        x1T = sb("x1T", [P, DC, GT])
        cw_s = sb("cw_s", [P, NW, DC, D])
        cT = sb("cT", [P, DC, GT])
        ctok = sb("ctok", [P, TG, D])
        Ls = sb("Ls", [P, TG, E])
        Lm = sb("Lm", [P, TG, E])
        v8 = sb("v8", [P, TG, 8])
        i8 = sb("i8", [P, TG, 8], U32)
        i8f = sb("i8f", [P, TG, 8])
        v8m = sb("v8m", [P, TG, 8])
        zs = sb("zs", [P, TG])
        s6 = sb("s6", [P, TG])
        OH = sb("OH", [P, TOPK, TG * E])
        M = sb("M", [P, TG * E], BF16)
        mc = sb("mc", [P, TG + 1, E], BF16)
        sa = sb("sa", [P, TG * E])
        sbb = sb("sbb", [P, TG * E])
        sc = sb("sc", [P, TG * E])
        slf = sb("slf", [P, TOPK, TG])
        sli = sb("sli", [P, TOPK, TG], I32)
        pair = sb("pair", [P, TG, TOPK, 2], I32)
        sil = sb("sil", [P, len(SCH), GT])
        hs = sb("hs", [P, len(SCH), GT])
        lst = sb("lst", [P, E * TJ, 2], I32)
        wb = sb("wb", [P, 2, WROW])
        wt = sb("wt", [FT, 2, D])
        ids = sb("ids", [P, UE, TJ], I32)
        wcol = sb("wcol", [P, UE, TJ])
        xg = sb("xg", [P, 2, TJ, D])
        xgT = sb("xgT", [P, 2, DC, CAP])
        sg = sb("sg", [P, 2, CAP])
        hh = sb("hh", [P, 2, 2, CAP])
        yo = sb("yo", [P, 2, TJ, D])
        yin = [t[:, 0:TJ * TG * D].rearrange("p (j t d) -> p j t d", j=TJ, d=D)
               for t in (cT_all[:, :, :].rearrange("p k n -> p (k n)"), cw_s[:, :, :, :].rearrange("p s k n -> p (s k n)"))]

        bank = [ctx.enter_context(nc.psum_tensor(f"bank{i}", [P, 512], F32)) for i in range(8)]
        bankb = bank[1][:, :].bitcast(BF16)

        def gcol(b, k, lo, n):
            o = k * (FR + CU + FT + FR) + lo
            return wb[:, b, o:o + n]

        def g_first(b, k): return gcol(b, k, 0, FR)
        def rest(b, k): return gcol(b, k, FR, CU + FT)
        def u_first(b, k): return gcol(b, k, FR + CU + FT, FR)
        def down_first(b): return wb[:, b, WROW - D:WROW]

        s_tick = sem("tick")
        s_const = sem("consts_made")
        s_dve0 = sem("dve_setup")
        s_ids = sem("ids_loaded")
        s_wall = sem("mix_weights_loaded")
        s_w = sem("layer_weights_loaded")
        s_ws = sem("shared_weights_loaded")
        s_init = sem("scratch_initialised")
        s_cbp = sem("cond_bias_in_psum")
        s_cbT = sem("cond_bias_ready")
        s_x = sem("x_loaded")
        s_xT = sem("xT_loaded")
        s_pf = sem("pairs_free")
        s_mix = sem("mixed_in_psum")
        s_h0 = sem("h0_ready")
        s_hp = sem("hidden_in_psum")
        s_h = sem("hidden_ready")
        s_vx = sem("vx_in_psum")
        s_lp = sem("mixture_logits_in_psum")
        s_lr = sem("mixture_logits_read")
        s_e = sem("mixture_exp_in")
        s_eo = sem("mixture_exp_out")
        s_al = sem("alpha_split")
        s_aTp = sem("alphaT_in_psum")
        s_aT = sem("alphaT_ready")
        s_sp = sem("spread_in_psum")
        s_spr = sem("spread_ready")
        s_z = sem("z_ready")
        s_up = sem("u_in_psum")
        s_x1 = sem("x1_ready")
        s_x1p = sem("x1_rows_in_psum")
        s_base = sem("base_ready")
        s_cw = [sem(f"cond_weights_loaded{i}") for i in range(NW)]
        s_cwf = sem("cond_weights_used")
        s_c = sem("cond_ready")
        s_call = sem("cond_kept")
        s_cv = sem("sums_chain")
        s_ctp = sem("cond_rows_in_psum")
        s_ct = sem("cond_rows_ready")
        s_rows = sem("cond_rows_stored")
        s_rp = sem("router_logits_in_psum")
        s_rr = sem("router_logits_read")
        s_m8 = sem("router_shifted")
        s_m8e = sem("router_exp_out")
        s_M = sem("choice_mask_ready")
        s_rk = sem("rank_in_psum")
        s_rkr = sem("rank_read")
        s_pair = sem("pairs_ready")
        s_scat = sem("pairs_scattered")
        s_v = sem("vector_chain")
        s_sh = sem("shared_in_psum")
        s_sil = sem("shared_silu_ready")
        s_hs = sem("shared_hidden_ready")
        s_sdp = sem("shared_down_in_psum")
        s_sb = sem("shared_added")
        s_lst = sem("slot_table_loaded")
        s_wb = [sem(f"expert_weights_loaded{i}") for i in range(2)]
        s_ids2 = sem("slot_ids_copied")
        s_xg = [sem(f"tokens_gathered{i}") for i in range(2)]
        s_xp = sem("tokensT_in_psum")
        s_xs = sem("tokensT_ready_scalar")
        s_xv = sem("tokensT_ready_vector")
        s_gu = sem("gate_up_in_psum")
        s_sg = sem("silu_ready")
        s_hh = sem("expert_hidden_ready")
        s_dp = sem("down_in_psum")
        s_ys = sem("rows_ready_scalar")
        s_yv = sem("rows_ready_vector")
        s_acc = [sem(f"rows_added{j}") for j in range(TJ)]
        s_yin = [sem(f"sums_loaded{j}") for j in range(2)]
        s_fin = sem("output_ready")
        s_out = sem("output_stored")

        block = ctx.enter_context(nc.Block())
        ACC0 = 16
        PV = 28

        @block.sync
        def _(sp):
            sp.dma_start(i_q0[:, :], idq0).then_inc(s_ids, 16)
            sp.dma_start(i_b0[:, :], idb0).then_inc(s_ids, 16)
            sp.dma_start(i_b1[:, :], idb1).then_inc(s_ids, 16)
            for q in range(BT):
                sp.dma_start(wall[q * S:(q + 1) * S, :, :], w0.rearrange("n c d -> c n d")).then_inc(s_wall, 16)
            sp.dma_start(fs_s[:, :], fs0).then_inc(s_wall, 16)
            sp.dma_start(x_g[:, :, :], x[0:GT, :].rearrange("(t p) d -> p t d", p=P)).then_inc(s_x, 16)
            sp.dma_start(W1s[:, :, :], W1.rearrange("(k p) n -> p k n", p=P)).then_inc(s_w, 16)
            sp.dma_start(b1s[:, :], b1).then_inc(s_w, 16)
            sp.dma_start(W2s[:, :, :], W2.rearrange("(k p) n -> p k n", p=P)).then_inc(s_w, 16)
            sp.dma_start(b2s[:, :], b2.rearrange("(a n) -> a n", a=1).to_broadcast([P, K0])).then_inc(s_w, 16)
            sp.dma_start(VTs[:, :, :], VT.rearrange("(k p) n -> p k n", p=P)).then_inc(s_w, 16)
            sp.dma_start(xT_g[:, :, :], xT[:, 0:GT].rearrange("(k p) n -> p k n", p=P)).then_inc(s_xT, 16)
            sp.dma_start(UTs[:, :, :], UT.rearrange("(k p) n -> p k n", p=P)).then_inc(s_w, 16)
            sp.dma_start(cbs[:, :], cb).then_inc(s_w, 16)
            sp.dma_start(gTs[:, :, :], gT.rearrange("(k p) n -> p k n", p=P)).then_inc(s_w, 16)

            def cond_weights(n, slot):
                which = sp.value_load(i_b1[0:1, bass.ds(n, 1)], min_val=0, max_val=NS1 - 1)
                sp.dma_start(cw_s[:, slot, :, :], cW[bass.ds(which, 1), :, :].rearrange("a (k p) n -> p (a k) n", p=P))\
                  .then_inc(s_cw[slot], 16)

            sp.wait_ge(s_ids, 48)
            for n in range(NW):
                cond_weights(n, n)
            sp.dma_start(sgus[:, :, :, :], sgu.rearrange("(k p) a n -> p k a n", p=P)).then_inc(s_ws, 16)
            for c, (lo, n) in enumerate(SCH):
                sp.dma_start(sds[0:n, c, :], sd[lo:lo + n, :]).then_inc(s_ws, 16)
            sp.wait_ge(s_const, 4)
            sp.dma_start(table.rearrange("(p n) c -> p (n c)", p=P), linit[:, :, :].rearrange("p n c -> p (n c)")).then_inc(s_init, 16)
            sp.dma_start(rows[N:N + P, :], zrow[:, :]).then_inc(s_init, 16)

            def group(g, last):
                if not last:
                    sp.wait_ge(s_mix, 2 * g + 2)
                    sp.sem_inc(s_tick, 1)
                    sp.dma_start(x_g[:, :, :], x[bass.ds((g + 1) * GT, GT), :].rearrange("(t p) d -> p t d", p=P)).then_inc(s_x, 16)
                    sp.wait_ge(s_x1, 2 * g + 2)
                    sp.sem_inc(s_tick, 1)
                    sp.dma_start(xT_g[:, :, :], xT[:, bass.ds((g + 1) * GT, GT)].rearrange("(k p) n -> p k n", p=P)).then_inc(s_xT, 16)
                for m in range(BG - NW if last else BG):
                    sp.wait_ge(s_cwf, g * BG + m + 1)
                    sp.sem_inc(s_tick, 1)
                    cond_weights(g * BG + m + NW, m % NW)
                sp.wait_ge(s_ct, 2 * g + 2)
                sp.sem_inc(s_tick, 1)
                sp.dma_start(rows[bass.ds(g * GT, GT), :].rearrange("(t p) d -> p t d", p=P), ctok[:, :, :]).then_inc(s_rows, 16)

            with sp.Fori(0, G - 1) as g:
                group(g, False)
            group(G - 1, True)

            def weights(e, b):
                sp.dma_start(wb[:, b, :], wblk[bass.ds(e, 1), :, :].rearrange("a p n -> p (a n)")).then_inc(s_wb[b], 16)
                sp.dma_start(wt[:, b, :], wdt[bass.ds(e, 1), :, :].rearrange("a p n -> p (a n)")).then_inc(s_wb[b], 16)

            weights(0, 0)
            weights(1, 1)
            sp.wait_ge(s_scat, 16 * TOPK * TT)
            sp.dma_start(lst[:, :, :].rearrange("p n c -> p (n c)"), table.rearrange("(p n) c -> p (n c)", p=P)).then_inc(s_lst, 16)
            with sp.Fori(0, E // 2 - 1) as i:
                for b in range(2):
                    sp.wait_ge(s_dp, TJ * (2 * i + b + 1))
                    sp.sem_inc(s_tick, 1)
                    weights(2 * i + b + 2, b)
            for q in range(G):
                for j in range(TJ):
                    if q == 0:
                        sp.wait_ge(s_acc[j], ACC0 + 16 * E)
                if q >= 2:
                    sp.wait_ge(s_fin, q - 1)
                for j in range(TJ):
                    sp.dma_start(yin[q % 2][:, j, :, :], acc[j][q * GT:(q + 1) * GT, :].rearrange("(t p) d -> p t d", p=P)).then_inc(s_yin[q % 2], 16)
                if q >= 1:
                    sp.wait_ge(s_fin, q)
                    sp.dma_start(out[(q - 1) * GT:q * GT, :].rearrange("(t p) d -> p t d", p=P), base[:, (q - 1) * TG:q * TG, :]).then_inc(s_out, 16)
            sp.wait_ge(s_fin, G)
            sp.dma_start(out[(G - 1) * GT:G * GT, :].rearrange("(t p) d -> p t d", p=P), base[:, (G - 1) * TG:G * TG, :]).then_inc(s_out, 16)
            sp.wait_ge(s_out, 16 * G)

        @block.gpsimd
        def _(pool):
            pool.sem_inc(s_pf, 1)
            pool.memset(zrow[:, :], 0.0)
            pool.memset(linit[:, :, :], 0)
            pool.memset(ident[:, :], 0.0)
            pool.memset(tri[:, :], 1.0)
            pool.memset(sel[:, :], 1.0)
            pool.memset(onesb[:, :], 1.0)
            pool.memset(ones8[:, :], 1.0)
            pool.iota(e_off_i[:, :], [[TJ, E]], base=0, channel_multiplier=0)
            pool.iota(iota_i[:, :], [[1, E]], base=0, channel_multiplier=0)
            pool.iota(pcol_i[:, :], [[0, 1]], base=0, channel_multiplier=1)
            pool.iota(tokid[:, :], [[P, TT]], base=0, channel_multiplier=1).then_inc(s_const, 1)
            pool.wait_ge(s_const, 1)
            pool.affine_select(out=ident[:, :], in_=ident[:, :], compare_op=ALU.not_equal, fill=1.0, base=0,
                               pattern=[[-1, P]], channel_multiplier=1)
            pool.affine_select(out=tri[:, :], in_=tri[:, :], compare_op=ALU.is_gt, fill=0.0, base=0,
                               pattern=[[1, P]], channel_multiplier=-1).then_inc(s_const, 1)
            selv = sel[:, :].rearrange("p (k r) -> p k r", r=R0)
            pool.affine_select(out=selv, in_=selv, compare_op=ALU.is_ge, fill=0.0, base=0,
                               pattern=[[-3, K0], [0, R0]], channel_multiplier=1)
            pool.iota(linit[:, :, 0], [[0, E * TJ]], base=N, channel_multiplier=1).then_inc(s_const, 1)
            pool.wait_ge(s_const, 3)
            pool.affine_select(out=selv, in_=selv, compare_op=ALU.is_ge, fill=0.0, base=2,
                               pattern=[[3, K0], [0, R0]], channel_multiplier=-1)
            pool.tensor_copy(identb[:, :], ident[:, :]).then_inc(s_const, 1)

            for j in range(TJ):
                pool.dma_start(acc[j].rearrange("(p r) d -> p r d", p=P),
                               zrow[:, :].unsqueeze(1).to_broadcast([P, (N + P) // P, D])).then_inc(s_acc[j], 16)
            pool.wait_ge(s_init, 32)
            with pool.Fori(0, G) as g:
                pool.wait_ge(s_pair, g + 1)
                pool.sem_inc(s_tick, 1)
                for t in range(TG):
                    for k in range(TOPK):
                        pool.indirect_dma_start(table, bass.IndirectOffsetOnAxis(sli[:, k, t:t + 1], 0),
                                                pair[:, t, k, :], None, bounds_check=LROWS - 1, oob_is_err=False)\
                            .then_inc(s_scat, 16)
                pool.wait_ge(s_scat, (g + 1) * 16 * TOPK * TG)
                pool.sem_inc(s_pf, 1)

            def gathers(e, u):
                b = u % 2
                pool.tensor_copy(ids[:, u % UE, :], lst[:, bass.ds(e * TJ, TJ), 0]).then_inc(s_ids2, 1)
                pool.tensor_copy(wcol[:, u % UE, :], lst[:, bass.ds(e * TJ, TJ), 1].bitcast(F32)).then_inc(s_ids2, 1)
                pool.wait_ge(s_ids2, 2 * e + 2)
                pool.sem_inc(s_tick, 1)
                for j in range(TJ):
                    pool.indirect_dma_start(xg[:, b, j, :], None, rows, bass.IndirectOffsetOnAxis(ids[:, u % UE, j:j + 1], 0))\
                        .then_inc(s_xg[b], 16)

            def scatters(e, u):
                for j in range(TJ):
                    if j == 0:
                        pool.wait_ge(s_ys, e + 2)
                        pool.sem_inc(s_tick, 1)
                    else:
                        pool.wait_ge(s_yv, 2 * e + j + 2)
                    pool.wait_ge(s_acc[j], ACC0 + 16 * e)
                    pool.sem_inc(s_tick, 1)
                    pool.indirect_dma_start(acc[j], bass.IndirectOffsetOnAxis(ids[:, u % UE, j:j + 1], 0),
                                            yo[:, u % 2, j, :], None, compute_op=ALU.add).then_inc(s_acc[j], 16)

            pool.wait_ge(s_lst, 16)
            pool.wait_ge(s_rows, 16 * G)
            gathers(0, 0)

            def experts(e0, last):
                for u in range(UE):
                    e = e0 + u
                    if not (last and u == UE - 1):
                        pool.wait_ge(s_xp, 2 * e + 2)
                        pool.sem_inc(s_tick, 1)
                        gathers(e + 1, u + 1)
                    scatters(e, u)

            with pool.Fori(0, E // UE - 1) as i:
                experts(i * UE, False)
            experts(E - UE, True)

        @block.scalar
        def _(act):
            act.sem_inc(s_ys, 1)
            act.wait_ge(s_cbp, 1)
            act.activation(cbT[:, :, :].rearrange("p k b -> p (k b)"), bank[7][:, 0:DC * B], ACT.Copy).then_inc(s_cbT, 1)
            with act.Fori(0, G) as g:
                act.wait_ge(s_mix, 2 * g + 1)
                act.activation(h0T[:, 0, :], bank[0][:, :], ACT.Copy).then_inc(s_h0, 1)
                for c in range(DC):
                    act.wait_ge(s_hp, 2 * g + 1 + c)
                    act.activation(hT[:, c, :], bank[2 + c][:, :], ACT.Relu, bias=b1s[:, c:c + 1]).then_inc(s_h, 1)
                act.wait_ge(s_e, g + 1)
                act.activation(alp[:, :, :], lg[:, :, :], ACT.Exp).then_inc(s_eo, 1)
                act.wait_ge(s_aTp, g + 1)
                act.activation(alT[:, :], bankb[0:3 * K0, 0:GT], ACT.Copy).then_inc(s_aT, 1)
                for c in range(KC):
                    act.wait_ge(s_sp, KC * g + c + 1)
                    if c >= 2:
                        act.wait_ge(s_z, KC * g + c - 1)
                    act.activation(spread[:, c % 2, :], bank[2 + c % 2][:, :], ACT.Copy).then_inc(s_spr, 1)
                for h in range(2):
                    act.wait_ge(s_x1p, 2 * g + h + 1)
                    act.activation(base[:, bass.ds(g * TG + 2 * h, 2), :],
                                   bank[4 + h][:, :].rearrange("p (t d) -> p t d", d=D), ACT.Copy).then_inc(s_base, 1)
                act.wait_ge(s_c, 2 * g + 2)
                act.activation(cT_all[:, :, bass.ds(g * GT, GT)], cT[:, :, :], ACT.Copy).then_inc(s_call, 1)
                for h in range(2):
                    act.wait_ge(s_ctp, 2 * g + h + 1)
                    act.activation(ctok[:, 2 * h:2 * h + 2, :].rearrange("p t d -> p (t d)"), bank[h][:, :], ACT.Copy).then_inc(s_ct, 1)
                act.wait_ge(s_m8, g + 1)
                act.activation(Lm[:, :, :], Lm[:, :, :], ACT.Exp).then_inc(s_m8e, 1)
                act.activation(v8m[:, :, :], v8m[:, :, :], ACT.Exp).then_inc(s_m8e, 1)
                act.wait_ge(s_rows, 16 * g + 16)
            with act.Fori(0, G) as g:
                for c, (lo, n) in enumerate(SCH):
                    act.wait_ge(s_sh, len(SCH) * g + c + 1)
                    act.activation(sil[0:n, c, :], bank[2 * c][0:n, :], ACT.Silu).then_inc(s_sil, 1)

            def tokens(e, u):
                act.wait_ge(s_xp, 2 * e + 1)
                act.activation(xgT[:, u % 2, 0, :], bank[0][:, 0:CAP], ACT.Copy).then_inc(s_xs, 1)

            def expert(e, u, last):
                act.wait_ge(s_gu, 3 * e + 1)
                act.activation(sg[:, 0, :], bank[2][:, 0:CAP], ACT.Silu).then_inc(s_sg, 1)
                act.wait_ge(s_gu, 3 * e + 3)
                act.activation(sg[0:FT, 1, :], bank[4][0:FT, 0:CAP], ACT.Silu).then_inc(s_sg, 1)
                if not last:
                    tokens(e + 1, u + 1)
                act.wait_ge(s_ids2, 2 * e + 2)
                act.wait_ge(s_acc[0], ACC0 - 16 + 16 * e)
                act.wait_ge(s_dp, TJ * e + 1)
                act.activation(yo[:, u % 2, 0, :], bank[5][:, 0:D], ACT.Copy, scale=wcol[:, u % UE, 0:1]).then_inc(s_ys, 1)

            tokens(0, 0)
            with act.Fori(0, E // UE - 1) as i:
                for u in range(UE):
                    expert(i * UE + u, u, False)
            for u in range(UE):
                expert(E - UE + u, u, u == UE - 1)

        @block.vector
        def _(dve):
            v = nc.vector
            done = [0, 0]

            def link(ins, g=0):
                done[1] += 1
                ins.then_inc(s_v, 1)
                dve.wait_ge(s_v, g * PV + (done[0] + done[1]))

            dve.sem_inc(s_yv, 2)
            v.memset(mc[:, :, :], 0.0)
            v.memset(gath0[:, :, :], 0.0)
            v.memset(bd[:, :, :], 0.0)
            dve.wait_ge(s_const, 1)
            v.tensor_copy(iota64[:, :], iota_i[:, :])
            v.tensor_copy(e_off[:, :], e_off_i[:, :])
            link(v.tensor_copy(pcol[:, :], pcol_i[:, :]))
            dve.wait_ge(s_ids, 48)
            v.tensor_copy(f_q0[:, :], i_q0[:, :])
            v.tensor_copy(f_b0[:, :], i_b0[:, :])
            link(v.tensor_copy(f_b1[:, :], i_b1[:, :]))
            v.tensor_scalar(oh1[:, :], f_b1[:, :], pcol[0:NS1, 0:1], None, ALU.is_equal).then_inc(s_dve0, 1)
            link(v.tensor_scalar(f_b0[:, :], f_b0[:, :], pcol[0:NS0, 0:1], None, ALU.is_equal))
            dve.wait_ge(s_wall, 16 * (BT + 1))
            v.tensor_tensor(bias0[:, :, :], f_b0[:, :].unsqueeze(2).to_broadcast([NS0, B, S]),
                            fs_s[:, :].unsqueeze(1).to_broadcast([NS0, B, S]), ALU.mult)
            for n in range(NS0):
                last = v.tensor_scalar(maskq[:, n, :], f_q0[:, :], float(n), None, ALU.is_equal)
            link(last)
            for n in range(NS0):
                link(v.copy_predicated(gath0[:, :, :], maskq[:, n, :].unsqueeze(2).to_broadcast([P, TT, S]),
                                       wall[:, n, :].unsqueeze(1).to_broadcast([P, TT, S])))
            for q in range(BT):
                last = v.tensor_copy(bd[q * S:(q + 1) * S, :, q * S:(q + 1) * S], gath0[q * S:(q + 1) * S, :, :])
            last.then_inc(s_dve0, 1)
            done[0], done[1] = done[1], 0

            with dve.Fori(0, G) as g:
                done[1] = 0
                dve.wait_ge(s_mix, 2 * g + 2)
                v.tensor_copy(h0T[:, 1, :], bank[1][:, :]).then_inc(s_h0, 1)
                dve.wait_ge(s_lp, g + 1)
                link(v.tensor_tensor(lg[:, :, :], bank[0][:, 0:TG * K0].rearrange("p (t k) -> p t k", k=K0),
                                     b2s[:, :].unsqueeze(1).to_broadcast([P, TG, K0]), ALU.add), g)
                link(v.reduce_max(lgm[:, :], lg[:, :, :], AX.X), g)
                v.tensor_tensor(lg[:, :, :], lg[:, :, :], lgm[:, :].unsqueeze(2).to_broadcast([P, TG, K0]),
                                ALU.subtract).then_inc(s_e, 1)
                dve.wait_ge(s_eo, g + 1)
                link(v.reduce_sum(lgm[:, :], alp[:, :, :], AX.X), g)
                link(v.reciprocal(lgm[:, :], lgm[:, :]), g)
                link(v.tensor_tensor(alp[:, :, :], alp[:, :, :], lgm[:, :].unsqueeze(2).to_broadcast([P, TG, K0]), ALU.mult), g)
                link(v.tensor_copy(als[:, :, :, 0], alp[:, :, :]), g)
                link(v.tensor_tensor(alr[:, :, :], alp[:, :, :], als[:, :, :, 0], ALU.subtract), g)
                link(v.tensor_copy(als[:, :, :, 1], alr[:, :, :]), g)
                link(v.tensor_tensor(alr[:, :, :], alr[:, :, :], als[:, :, :, 1], ALU.subtract), g)
                v.tensor_copy(als[:, :, :, 2], alr[:, :, :]).then_inc(s_al, 1)
                for c in range(KC):
                    dve.wait_ge(s_vx, KC * g + c + 1)
                    dve.wait_ge(s_spr, KC * g + c + 1)
                    v.tensor_tensor(z[:, c, :], spread[:, c % 2, :], bank[4 + c][:, :], ALU.mult).then_inc(s_z, 1)
                dve.wait_ge(s_xT, 16 * g + 16)
                for c in range(DC):
                    dve.wait_ge(s_up, DC * g + c + 1)
                    v.tensor_tensor(x1T[:, c, :], xT_g[:, c, :], bank[c][:, :], ALU.add).then_inc(s_x1, 1)
                dve.wait_ge(s_cbT, 1)
                dve.wait_ge(s_cwf, BG * g + BG)
                for c in range(DC):
                    v.tensor_tensor(cT[:, c, :].rearrange("p (b s) -> p b s", s=S),
                                    bank[6 + c][:, :].rearrange("p (b s) -> p b s", s=S),
                                    cbT[:, c, bass.ds(g * BG, BG)].unsqueeze(2).to_broadcast([P, BG, S]), ALU.add).then_inc(s_c, 1)
                dve.wait_ge(s_rp, g + 1)
                link(v.tensor_copy(Ls[:, :, :].rearrange("p t e -> p (t e)"), bank[2][:, 0:TG * E]), g)
                dve.sem_inc(s_tick, 1)
                for t in range(TG):
                    last = v.max(v8[:, t, :], Ls[:, t, :])
                link(last, g)
                v.tensor_tensor(Lm[:, :, :], Ls[:, :, :], v8[:, :, 0:1].to_broadcast([P, TG, E]), ALU.subtract)
                v.tensor_tensor(v8m[:, :, :], v8[:, :, :], v8[:, :, 0:1].to_broadcast([P, TG, 8]), ALU.subtract).then_inc(s_m8, 1)
                for t in range(TG):
                    last = v.max_index(i8[:, t, :], v8[:, t, :], Ls[:, t, :])
                link(last, g)
                v.tensor_copy(mc[:, 0, :], mc[:, TG, :])
                link(v.tensor_copy(i8f[:, :, :], i8[:, :, :]), g)
                for k in range(TOPK):
                    last = v.tensor_tensor(OH[:, k, :].rearrange("p (t e) -> p t e", e=E),
                                           iota64[:, :].unsqueeze(1).to_broadcast([P, TG, E]),
                                           i8f[:, :, k:k + 1].to_broadcast([P, TG, E]), ALU.is_equal)
                link(last, g)
                with nc.allow_low_precision(reason="counts up to 16 are exact"):
                    link(v.reduce_sum(M[:, :], OH[:, :, :].rearrange("p k n -> p n k"), AX.X), g)
                    for t in range(TG):
                        last = v.tensor_tensor(mc[:, t + 1, :], mc[:, t, :], M[:, t * E:(t + 1) * E], ALU.add)
                        if t < TG - 1:
                            link(last, g)
                last.then_inc(s_M, 1)
                dve.wait_ge(s_m8e, 2 * g + 2)
                link(v.reduce_sum(zs[:, :], Lm[:, :, :], AX.X), g)
                link(v.reciprocal(zs[:, :], zs[:, :]), g)
                link(v.tensor_tensor(v8m[:, :, :], v8m[:, :, :], zs[:, :].unsqueeze(2).to_broadcast([P, TG, 8]), ALU.mult), g)
                link(v.reduce_sum(s6[:, :], v8m[:, :, 0:TOPK], AX.X), g)
                link(v.tensor_scalar(s6[:, :], s6[:, :], 1e-20, None, ALU.add), g)
                link(v.reciprocal(s6[:, :], s6[:, :]), g)
                dve.wait_ge(s_pf, g + 1)
                v.tensor_tensor(pair[:, :, :, 1].bitcast(F32), v8m[:, :, 0:TOPK],
                                s6[:, :].unsqueeze(2).to_broadcast([P, TG, TOPK]), ALU.mult)
                v.tensor_copy(pair[:, :, :, 0], tokid[:, bass.ds(g * TG, TG)].unsqueeze(2).to_broadcast([P, TG, TOPK]))
                dve.wait_ge(s_rk, g + 1)
                v.tensor_scalar(sa[:, :], bank[3][:, 0:TG * E], float(P), float(1 - LROWS), ALU.is_ge, ALU.mult)
                v.tensor_scalar(sbb[:, :], bank[3][:, 0:TG * E], float(2 * P), float(1 - LROWS), ALU.is_ge, ALU.mult)
                v.scalar_tensor_tensor(sc[:, :].rearrange("p (t e) -> p t e", e=E), bank[3][:, 0:TG * E].rearrange("p (t e) -> p t e", e=E),
                                       float(E * TJ), e_off[:, :].unsqueeze(1).to_broadcast([P, TG, E]), ALU.mult, ALU.add).then_inc(s_rkr, 1)
                dve.wait_ge(s_rkr, g + 1)
                link(v.tensor_tensor(sa[:, :], sa[:, :], sbb[:, :], ALU.add), g)
                link(v.tensor_tensor(sc[:, :], sc[:, :], sa[:, :], ALU.add), g)
                link(v.tensor_tensor(OH[:, :, :], OH[:, :, :], sc[:, :].unsqueeze(1).to_broadcast([P, TOPK, TG * E]), ALU.mult), g)
                link(v.reduce_sum(slf[:, :, :], OH[:, :, :].rearrange("p k (t e) -> p k t e", e=E), AX.X), g)
                v.tensor_copy(sli[:, :, :], slf[:, :, :]).then_inc(s_pair, 1)
                assert done[1] == PV, done

            dve.wait_ge(s_base, 2 * G)
            with dve.Fori(0, G) as g:
                for c, (lo, n) in enumerate(SCH):
                    dve.wait_ge(s_sil, len(SCH) * g + c + 1)
                    v.tensor_tensor(hs[0:n, c, :], sil[0:n, c, :], bank[2 * c + 1][0:n, :], ALU.mult).then_inc(s_hs, 1)
                for h in range(2):
                    dve.wait_ge(s_sdp, 2 * g + h + 1)
                    rows2 = base[:, bass.ds(g * TG + 2 * h, 2), :]
                    v.tensor_tensor(rows2, rows2, bank[6 + h][:, :].rearrange("p (t d) -> p t d", d=D), ALU.add).then_inc(s_sb, 1)

            def tokens(e, u):
                dve.wait_ge(s_xp, 2 * e + 2)
                v.tensor_copy(xgT[:, u % 2, 1, :], bank[1][:, 0:CAP]).then_inc(s_xv, 1)

            def expert(e, u, last):
                dve.wait_ge(s_sg, 2 * e + 1)
                dve.wait_ge(s_gu, 3 * e + 2)
                v.tensor_tensor(hh[:, u % 2, 0, :], sg[:, 0, :], bank[3][:, 0:CAP], ALU.mult).then_inc(s_hh, 1)
                dve.wait_ge(s_sg, 2 * e + 2)
                v.tensor_tensor(hh[0:FT, u % 2, 1, :], sg[0:FT, 1, :], bank[4][CU:CU + FT, 0:CAP], ALU.mult).then_inc(s_hh, 1)
                if not last:
                    tokens(e + 1, u + 1)
                dve.wait_ge(s_ids2, 2 * e + 2)
                for j in range(1, TJ):
                    dve.wait_ge(s_acc[j], ACC0 - 16 + 16 * e)
                    dve.wait_ge(s_dp, TJ * e + j + 1)
                    v.tensor_scalar(yo[:, u % 2, j, :], bank[5 + j][:, 0:D], wcol[:, u % UE, j:j + 1], None, ALU.mult).then_inc(s_yv, 1)

            tokens(0, 0)
            with dve.Fori(0, E // UE - 1) as i:
                for u in range(UE):
                    expert(i * UE + u, u, False)
            for u in range(UE):
                expert(E - UE + u, u, u == UE - 1)

            for q in range(G):
                dve.wait_ge(s_yin[q % 2], 16 * TJ * (q // 2 + 1))
                part = base[:, q * TG:(q + 1) * TG, :]
                for j in range(TJ):
                    last = v.tensor_tensor(part, part, yin[q % 2][:, j, :, :], ALU.add)
                    if j < TJ - 1:
                        last.then_inc(s_cv, 1)
                        dve.wait_ge(s_cv, q * (TJ - 1) + j + 1)
                last.then_inc(s_fin, 1)

        @block.tensor
        def _(pe):
            mm, tr = nc.tensor.matmul, nc.tensor.transpose
            pe.wait_ge(s_w, 16 * 8)
            pe.wait_ge(s_dve0, 2)
            pe.wait_ge(s_const, 4)
            for c in range(DC):
                last = mm(bank[7][:, c * B:(c + 1) * B], cbs[:, c * P:(c + 1) * P], oh1[:, :], start=True, stop=True)
            last.then_inc(s_cbp, 1)
            pe.wait_ge(s_cbT, 1)
            with pe.Fori(0, G) as g:
                pe.wait_ge(s_x, 16 * g + 16)
                for c in range(DC):
                    for t in range(TG):
                        o = bank[c][:, t * P:(t + 1) * P]
                        mm(o, x_g[:, t, c * P:(c + 1) * P], bd[:, bass.ds(g * TG + t, 1), :].rearrange("p a n -> p (a n)"),
                           start=True, stop=False)
                        last = mm(o, ones8[:, :], bias0[:, bass.ds((g * TG + t) * BT, BT), :].rearrange("p b s -> p (b s)"),
                                  start=False, stop=True)
                    last.then_inc(s_mix, 1)
                pe.wait_ge(s_h0, 2 * g + 2)
                for o in range(DC):
                    for c in range(DC):
                        last = mm(bank[2 + o][:, :], W1s[:, c, o * P:(o + 1) * P], h0T[:, c, :], start=c == 0, stop=c == DC - 1)
                    last.then_inc(s_hp, 1)

                def vx(o):
                    for c in range(DC):
                        last = mm(bank[4 + o][:, :], VTs[:, c, o * P:(o + 1) * P], h0T[:, c, :], start=c == 0, stop=c == DC - 1)
                    last.then_inc(s_vx, 1)

                vx(0)
                pe.wait_ge(s_h, 2 * g + 2)
                for t in range(TG):
                    for c in range(DC):
                        last = mm(bank[0][:, t * K0:(t + 1) * K0], hT[:, c, t * P:(t + 1) * P], W2s[:, c, :],
                                  start=c == 0, stop=c == DC - 1)
                last.then_inc(s_lp, 1)
                for o in range(1, KC):
                    vx(o)
                pe.wait_ge(s_al, g + 1)
                for t in range(TG):
                    last = tr(bankb[0:3 * K0, t * P:(t + 1) * P], als[:, t, :, :].rearrange("p k a -> p (k a)"), identb[:, :])
                last.then_inc(s_aTp, 1)
                pe.wait_ge(s_aT, g + 1)
                for c in range(KC):
                    if c >= 2:
                        pe.wait_ge(s_spr, KC * g + c - 1)
                    mm(bank[2 + c % 2][:, :], sel[:, c * P:(c + 1) * P], alT[:, :], start=True, stop=True).then_inc(s_sp, 1)
                pe.wait_ge(s_z, KC * g + KC)
                for o in range(DC):
                    for c in range(KC):
                        last = mm(bank[o][:, :], UTs[:, c, o * P:(o + 1) * P], z[:, c, :], start=c == 0, stop=c == KC - 1)
                    last.then_inc(s_up, 1)
                pe.wait_ge(s_x1, 2 * g + 2)
                for t in range(TG):
                    for c in range(DC):
                        last = tr(bank[4 + t // 2][:, (t % 2) * D + c * P:(t % 2) * D + (c + 1) * P], x1T[:, c, t * P:(t + 1) * P], ident[:, :])
                    if t % 2:
                        last.then_inc(s_x1p, 1)
                for m in range(BG):
                    pe.wait_ge(s_cw[m % NW], 16 * (BG // NW * g + m // NW + 1))
                    for o in range(DC):
                        for c in range(DC):
                            last = mm(bank[6 + o][:, m * S:(m + 1) * S], cw_s[:, m % NW, c, o * P:(o + 1) * P],
                                      x1T[:, c, m * S:(m + 1) * S], start=c == 0, stop=c == DC - 1)
                    last.then_inc(s_cwf, 1)
                pe.wait_ge(s_c, 2 * g + 2)
                for t in range(TG):
                    for c in range(DC):
                        last = mm(bank[2][:, t * E:(t + 1) * E], cT[:, c, t * P:(t + 1) * P], gTs[:, c, :], start=c == 0, stop=c == DC - 1)
                last.then_inc(s_rp, 1)
                for t in range(TG):
                    for c in range(DC):
                        last = tr(bank[t // 2][:, (t % 2) * D + c * P:(t % 2) * D + (c + 1) * P], cT[:, c, t * P:(t + 1) * P], ident[:, :])
                    if t % 2:
                        last.then_inc(s_ctp, 1)
                pe.wait_ge(s_M, g + 1)
                for t in range(TG):
                    mm(bank[3][:, t * E:(t + 1) * E], tri[:, :], M[:, t * E:(t + 1) * E], start=True, stop=False)
                    last = mm(bank[3][:, t * E:(t + 1) * E], onesb[:, :], mc[:, t, :], start=False, stop=True)
                last.then_inc(s_rk, 1)
                pe.wait_ge(s_ct, 2 * g + 2)
                pe.wait_ge(s_rkr, g + 1)
            pe.wait_ge(s_ws, 16 * (1 + len(SCH)))
            pe.wait_ge(s_call, G)
            with pe.Fori(0, G) as g:
                for s_, (lo, n) in enumerate(SCH):
                    for a in range(2):
                        for c in range(DC):
                            last = mm(bank[2 * s_ + a][0:n, :], sgus[:, c, a, lo:lo + n], cT_all[:, c, bass.ds(g * GT, GT)],
                                      start=c == 0, stop=c == DC - 1)
                    last.then_inc(s_sh, 1)
                pe.wait_ge(s_hs, len(SCH) * (g + 1))
                for t in range(TG):
                    for s_, (lo, n) in enumerate(SCH):
                        last = mm(bank[6 + t // 2][:, (t % 2) * D:(t % 2 + 1) * D], hs[0:n, s_, t * P:(t + 1) * P], sds[0:n, s_, :],
                                  start=s_ == 0, stop=s_ == len(SCH) - 1)
                    if t % 2:
                        last.then_inc(s_sdp, 1)
                pe.wait_ge(s_sb, 2 * g + 2)

            def run(e0, i2, last):
                for u in range(UE):
                    e = e0 + u
                    pe_expert(e, u, i2 + (u // 2 + 1), i2 + ((u + 1) // 2 + 1), last and u == UE - 1)

            def pe_expert(e, u, mine, nexts, last_one):
                b = u % 2
                pe.wait_ge(s_wb[b], 32 * mine)
                pe.wait_ge(s_xs, e + 1)
                pe.wait_ge(s_xv, e + 1)
                for o, w, n in ((2, g_first, FR), (3, u_first, FR), (4, rest, CU + FT)):
                    for c in range(DC):
                        last = mm(bank[o][0:n, 0:CAP], w(b, c), xgT[:, b, c, :], start=c == 0, stop=c == DC - 1)
                    last.then_inc(s_gu, 1)
                if not last_one:
                    pe_tokens(u + 1, nexts)
                pe.wait_ge(s_hh, 2 * e + 2)
                pe.wait_ge(s_ys, e + 1)
                pe.wait_ge(s_yv, 2 * e + 2)
                for j in range(TJ):
                    o = bank[5 + j][:, 0:D]
                    mm(o, hh[:, b, 0, j * P:(j + 1) * P], down_first(b), start=True, stop=False)
                    mm(o, hh[0:FT, b, 1, j * P:(j + 1) * P], wt[:, b, :], start=False, stop=True).then_inc(s_dp, 1)

            def pe_tokens(u, mine):
                b = u % 2
                pe.wait_ge(s_xg[b], 16 * TJ * mine)
                for c in range(DC):
                    for j in range(TJ):
                        last = tr(bank[c][:, j * P:(j + 1) * P], xg[:, b, j, c * P:(c + 1) * P], ident[:, :])
                    last.then_inc(s_xp, 1)

            pe_tokens(0, 1)
            with pe.Fori(0, E // UE - 1) as i:
                run(i * UE, i * (UE // 2), False)
            run(E - UE, (E - UE) // 2, True)


IN = ["x", "xT", "idq0", "idb0", "idb1", "w0", "fs0", "W1", "b1", "W2", "b2", "VT", "UT", "cW", "cb", "gT", "wblk", "wdt", "sgu", "sd"]


def kernel(x, itok_B_0_7, fside_8xS_0, itok_B_0_15, L0_cond_weights, L0_ffn_U, L0_ffn_V, L0_ffn_W1, L0_ffn_b1,
           L0_ffn_W2, L0_ffn_b2, L1_cond_W, L1_cond_b, L1_ffn_gate_w, L1_ffn_w_gate, L1_ffn_w_up, L1_ffn_w_down,
           L1_ffn_sh_gate, L1_ffn_sh_up, L1_ffn_sh_down):
    import numpy as np
    import concourse.bacc as bacc
    from concourse.bass_utils import run_bass_kernel_spmd

    x2 = np.asarray(x).reshape(N, D)
    ids0, ids1 = np.asarray(itok_B_0_7), np.asarray(itok_B_0_15)

    def packed(w_gate, w_up, w_down):
        g = np.asarray(w_gate).transpose(0, 2, 1).reshape(E, DC, P, F).transpose(0, 2, 1, 3)
        u = np.asarray(w_up).transpose(0, 2, 1).reshape(E, DC, P, F).transpose(0, 2, 1, 3)
        gap = np.zeros((E, P, DC, CU - FT), g.dtype)
        gu = np.concatenate([g, gap, u[..., FR:], u[..., :FR]], axis=3).reshape(E, P, WROW - D)
        d = np.asarray(w_down).transpose(0, 2, 1)
        return np.concatenate([gu, d[:, :FR]], axis=2), d[:, FR:]

    wblk, wdt = packed(L1_ffn_w_gate, L1_ffn_w_up, L1_ffn_w_down)
    arrays = {
        "x": x2, "xT": x2.T,
        "idq0": np.repeat(ids0.reshape(TT, BT).T, S, axis=0),
        "idb0": np.repeat(ids0.reshape(1, B), NS0, axis=0),
        "idb1": np.repeat(ids1.reshape(1, B), NS1, axis=0),
        "w0": L0_cond_weights, "fs0": fside_8xS_0,
        "W1": L0_ffn_W1, "b1": np.asarray(L0_ffn_b1).reshape(DC, P).T, "W2": L0_ffn_W2, "b2": L0_ffn_b2,
        "VT": np.asarray(L0_ffn_V).reshape(KR, D).T,
        "UT": np.asarray(L0_ffn_U).transpose(0, 2, 1).reshape(KR, D),
        "cW": L1_cond_W, "cb": L1_cond_b, "gT": np.asarray(L1_ffn_gate_w).T,
        "wblk": wblk, "wdt": wdt,
        "sgu": np.stack([np.asarray(L1_ffn_sh_gate).T, np.asarray(L1_ffn_sh_up).T], axis=1),
        "sd": np.asarray(L1_ffn_sh_down).T,
    }
    nc = bacc.Bacc("TRN2", target_bir_lowering=False, num_devices=1)
    aps = []
    for name in IN:
        a = np.ascontiguousarray(arrays[name])
        arrays[name] = a
        aps.append(nc.dram_tensor(f"in_{name}", a.shape, mybir.dt.from_np(a.dtype), kind="ExternalInput").ap())
    out = nc.dram_tensor("out_y", (N, D), F32, kind="ExternalOutput").ap()
    program(nc, *aps, out)
    r = run_bass_kernel_spmd(nc, [{f"in_{k}": a for k, a in arrays.items()}], core_ids=[0])
    return r.results[0]["out_y"].reshape(B, S, D)
```

```python
from contextlib import ExitStack

import concourse.bass as bass
from concourse import mybir

F32 = mybir.dt.float32
BF16 = mybir.dt.bfloat16
I32 = mybir.dt.int32
U32 = mybir.dt.uint32
ALU = mybir.AluOpType
ACT = mybir.ActivationFunctionType
AX = mybir.AxisListType

P = 128
B, S, D = 64, 32, 256
N = B * S
NS0, NS1 = 8, 16
K0, R0 = 8, 64
E, TOPK, F, FS = 64, 6, 176, 352
CAP = 2 * ((N * TOPK + E - 1) // E)
DC = D // P
G = 4
GT = N // G
TG = GT // P
TT = N // P
BG = B // G
BT = P // S
KR = K0 * R0
KC = KR // P
TJ = CAP // P
LROWS = P * E * TJ
FR, FT = P, F - P
CU = 64
WROW = DC * (FR + CU + FT + FR) + D
SCH = [(0, P), (P, P), (2 * P, FS - 2 * P)]
NW = 8
UE = 4
SIZES = [P, 3 * P // 2, 2 * P, 5 * P // 2, CAP]
SIZE, LANDED, GATHERED = range(3)
assert TJ * P == CAP and G * GT == N and BG % NW == 0


def program(nc, x, xT, idq0, idb0, idb1, w0, fs0, W1, b1, W2, b2, VT, UT, cW, cb, gT, wblk, wdt, sgu, sd, out):
    ctx = ExitStack()
    with ctx:
        def sb(name, shape, dt=F32):
            return ctx.enter_context(nc.sbuf_tensor(name, shape, dt))

        def sem(name):
            return ctx.enter_context(nc.semaphore(name))

        rows = nc.dram_tensor("token_rows", [N + P, D], F32).ap()
        table = nc.dram_tensor("slot_table", [LROWS, 2], I32).ap()
        acc = [nc.dram_tensor(f"acc{j}", [N + P, D], F32).ap() for j in range(TJ)]

        ident = sb("ident", [P, P])
        identb = sb("identb", [P, P], BF16)
        tri = sb("tri", [P, P], BF16)
        onesb = sb("onesb", [P, P], BF16)
        ones8 = sb("ones8", [NS0, P])
        sel = sb("sel", [3 * K0, KR], BF16)
        iota64 = sb("iota64", [P, E])
        e_off = sb("e_off", [P, E])
        pcol = sb("pcol", [P, 1])
        iota_i = sb("iota_i", [P, E], I32)
        e_off_i = sb("e_off_i", [P, E], I32)
        pcol_i = sb("pcol_i", [P, 1], I32)
        tokid = sb("tokid", [P, TT], I32)
        zrow = sb("zrow", [P, D])
        linit = sb("linit", [P, E * TJ, 2], I32)
        i_q0 = sb("i_q0", [P, TT], I32)
        f_q0 = sb("f_q0", [P, TT])
        i_b0 = sb("i_b0", [NS0, B], I32)
        i_b1 = sb("i_b1", [NS1, B], I32)
        f_b0 = sb("f_b0", [NS0, B])
        f_b1 = sb("f_b1", [NS1, B])
        oh1 = sb("oh1", [NS1, B])
        wall = sb("wall", [P, NS0, S])
        maskq = sb("maskq", [P, NS0, TT], U32)
        gath0 = sb("gath0", [P, TT, S])
        bd = sb("bd", [P, TT, P])
        fs_s = sb("fs_s", [NS0, S])
        bias0 = sb("bias0", [NS0, B, S])
        W1s = sb("W1s", [P, DC, D])
        b1s = sb("b1s", [P, DC])
        W2s = sb("W2s", [P, DC, K0])
        b2s = sb("b2s", [P, K0])
        VTs = sb("VTs", [P, DC, KR])
        UTs = sb("UTs", [P, KC, D])
        cbs = sb("cbs", [NS1, D])
        cbT = sb("cbT", [P, DC, B])
        gTs = sb("gTs", [P, DC, E])
        sgus = sb("sgus", [P, DC, 2, FS])
        sds = sb("sds", [P, len(SCH), D])
        base = sb("base", [P, TT, D])
        cT_all = sb("cT_all", [P, DC, N])
        x_g = sb("x_g", [P, TG, D])
        xT_g = sb("xT_g", [P, DC, GT])
        h0T = sb("h0T", [P, DC, GT])
        hT = sb("hT", [P, DC, GT])
        lg = sb("lg", [P, TG, K0])
        lgm = sb("lgm", [P, TG])
        alp = sb("alp", [P, TG, K0])
        alr = sb("alr", [P, TG, K0])
        als = sb("als", [P, TG, K0, 3], BF16)
        alT = sb("alT", [3 * K0, GT], BF16)
        spread = sb("spread", [P, 2, GT])
        z = sb("z", [P, KC, GT])
        x1T = sb("x1T", [P, DC, GT])
        cw_s = sb("cw_s", [P, NW, DC, D])
        cT = sb("cT", [P, DC, GT])
        ctok = sb("ctok", [P, TG, D])
        Ls = sb("Ls", [P, TG, E])
        Lm = sb("Lm", [P, TG, E])
        v8 = sb("v8", [P, TG, 8])
        i8 = sb("i8", [P, TG, 8], U32)
        i8f = sb("i8f", [P, TG, 8])
        v8m = sb("v8m", [P, TG, 8])
        zs = sb("zs", [P, TG])
        s6 = sb("s6", [P, TG])
        OH = sb("OH", [P, TOPK, TG * E])
        M = sb("M", [P, TG * E], BF16)
        mc = sb("mc", [P, TG + 1, E], BF16)
        sa = sb("sa", [P, TG * E])
        sbb = sb("sbb", [P, TG * E])
        sc = sb("sc", [P, TG * E])
        slf = sb("slf", [P, TOPK, TG])
        sli = sb("sli", [P, TOPK, TG], I32)
        pair = sb("pair", [P, TG, TOPK, 2], I32)
        sil = sb("sil", [P, len(SCH), GT])
        hs = sb("hs", [P, len(SCH), GT])
        lst = sb("lst", [P, (E + 1) * TJ, 2], I32)
        wb2 = sb("wb2", [P, 2, WROW])
        wt2 = sb("wt2", [FT, 2, D])
        wb = [wb2[:, 0, :], wb2[:, 1, :]] + [t[:, :, :].rearrange("p k n -> p (k n)")[:, 0:WROW] for t in (h0T, hT)]
        wt = [wt2[:, 0, :], wt2[:, 1, :]] + [spread[0:FT, i, 0:D] for i in range(2)]
        facts = sb("facts", [P, 3, E], I32)
        tiles_f = sb("tiles_f", [P, E])
        seen = sb("seen", [P, E])
        fl = sb("fl", [P, E])
        onesf = sb("onesf", [P, E])
        last_wait = sb("last_wait", [P, 1], I32)
        turns_i = sb("turns_i", [P, E], I32)
        turns = sb("turns", [P, E])
        more = sb("more", [P, len(SIZES) - 1, E])
        gids = sb("gids", [P, UE, TJ], I32)
        sids = sb("sids", [P, UE, TJ], I32)
        wcol = sb("wcol", [P, UE, TJ])
        xg = cw_s[:, :, :, :].rearrange("p s k n -> p (s k n)")[:, 0:UE * TJ * D]\
            .rearrange("p (u j d) -> p u j d", j=TJ, d=D)
        xgT = sb("xgT", [P, 2, DC, CAP])
        sg = sb("sg", [P, 2, CAP])
        hh = sb("hh", [P, 2, 2, CAP])
        yo = sb("yo", [P, 2, TJ, D])
        yin = [t[:, 0:TJ * TG * D].rearrange("p (j t d) -> p j t d", j=TJ, d=D)
               for t in (cT_all[:, :, :].rearrange("p k n -> p (k n)"), cw_s[:, :, :, :].rearrange("p s k n -> p (s k n)"))]

        bank = [ctx.enter_context(nc.psum_tensor(f"bank{i}", [P, 512], F32)) for i in range(8)]
        bankb = bank[1][:, :].bitcast(BF16)

        def gcol(b, k, lo, n):
            o = k * (FR + CU + FT + FR) + lo
            return wb[b][:, o:o + n]

        def g_first(b, k): return gcol(b, k, 0, FR)
        def rest(b, k): return gcol(b, k, FR, CU + FT)
        def u_first(b, k): return gcol(b, k, FR + CU + FT, FR)
        def down_first(b): return wb[b][:, WROW - D:WROW]

        s_tick = sem("tick")
        s_const = sem("consts_made")
        s_dve0 = sem("dve_setup")
        s_ids = sem("ids_loaded")
        s_wall = sem("mix_weights_loaded")
        s_w = sem("layer_weights_loaded")
        s_ws = sem("shared_weights_loaded")
        s_init = sem("scratch_initialised")
        s_cbp = sem("cond_bias_in_psum")
        s_cbT = sem("cond_bias_ready")
        s_x = sem("x_loaded")
        s_xT = sem("xT_loaded")
        s_pf = sem("pairs_free")
        s_mix = sem("mixed_in_psum")
        s_h0 = sem("h0_ready")
        s_hp = sem("hidden_in_psum")
        s_h = sem("hidden_ready")
        s_vx = sem("vx_in_psum")
        s_lp = sem("mixture_logits_in_psum")
        s_lr = sem("mixture_logits_read")
        s_e = sem("mixture_exp_in")
        s_eo = sem("mixture_exp_out")
        s_al = sem("alpha_split")
        s_aTp = sem("alphaT_in_psum")
        s_aT = sem("alphaT_ready")
        s_sp = sem("spread_in_psum")
        s_spr = sem("spread_ready")
        s_z = sem("z_ready")
        s_up = sem("u_in_psum")
        s_x1 = sem("x1_ready")
        s_x1p = sem("x1_rows_in_psum")
        s_base = sem("base_ready")
        s_cw = [sem(f"cond_weights_loaded{i}") for i in range(NW)]
        s_cwf = sem("cond_weights_used")
        s_c = sem("cond_ready")
        s_call = sem("cond_kept")
        s_cv = sem("sums_chain")
        s_ctp = sem("cond_rows_in_psum")
        s_ct = sem("cond_rows_ready")
        s_rows = sem("cond_rows_stored")
        s_rp = sem("router_logits_in_psum")
        s_rr = sem("router_logits_read")
        s_m8 = sem("router_shifted")
        s_m8e = sem("router_exp_out")
        s_M = sem("choice_mask_ready")
        s_rk = sem("rank_in_psum")
        s_rkr = sem("rank_read")
        s_pair = sem("pairs_ready")
        s_scat = sem("pairs_scattered")
        s_v = sem("vector_chain")
        s_sh = sem("shared_in_psum")
        s_sil = sem("shared_silu_ready")
        s_hs = sem("shared_hidden_ready")
        s_sdp = sem("shared_down_in_psum")
        s_sb = sem("shared_added")
        s_cnt = sem("choice_counts_in_psum")
        s_flags = sem("flags_ready")
        s_land = sem("rows_landed")
        s_fl = sem("flags_chain")
        s_lst = sem("slot_table_loaded")
        s_wb = [sem(f"expert_weights_loaded{i}") for i in range(UE)]
        s_gid = sem("gather_ids_copied")
        s_ids2 = sem("slot_ids_copied")
        s_xg = [sem(f"tokens_gathered{i}") for i in range(UE)]
        s_xp = sem("tokensT_in_psum")
        s_xs = sem("tokensT_ready_scalar")
        s_xv = sem("tokensT_ready_vector")
        s_gu = sem("gate_up_in_psum")
        s_sg = sem("silu_ready")
        s_hh = sem("expert_hidden_ready")
        s_dp = sem("down_in_psum")
        s_ys = sem("rows_ready_scalar")
        s_yv = sem("rows_ready_vector")
        s_acc0 = sem("rows_added_first_tiles")
        s_acc = sem("rows_added_other_tiles")
        s_yin = [sem(f"sums_loaded{j}") for j in range(2)]
        s_fin = sem("output_ready")
        s_out = sem("output_stored")

        def by_tiles(eng, size, work):
            with eng.If(size > 2):
                work(3)
            with eng.Else():
                with eng.If(size > 0):
                    work(2)
                with eng.Else():
                    work(1)

        def notes(eng):
            known = {}

            def get(what, e, u):
                if (what, u) not in known:
                    known[what, u] = eng.value_load(facts[0:1, what, bass.ds(e, 1)], min_val=0, max_val=16 * (TJ * E + TJ))
                return known[what, u]

            def start(e, u):
                if u == (E - UE + 1 if isinstance(e, int) else 1):
                    known.clear()
            return get, start

        def all_steps(eng, step):
            step(0, 0, first=True)
            with eng.Fori(0, E // UE - 1) as i:
                for u in range(1, UE + 1):
                    step(i * UE + u, u)
            for e in range(E - UE + 1, E):
                step(e, e)

        block = ctx.enter_context(nc.Block())
        PV = 28

        @block.sync
        def _(sp):
            sp.dma_start(i_q0[:, :], idq0).then_inc(s_ids, 16)
            sp.dma_start(i_b0[:, :], idb0).then_inc(s_ids, 16)
            sp.dma_start(i_b1[:, :], idb1).then_inc(s_ids, 16)
            for q in range(BT):
                sp.dma_start(wall[q * S:(q + 1) * S, :, :], w0.rearrange("n c d -> c n d")).then_inc(s_wall, 16)
            sp.dma_start(fs_s[:, :], fs0).then_inc(s_wall, 16)
            sp.dma_start(x_g[:, :, :], x[0:GT, :].rearrange("(t p) d -> p t d", p=P)).then_inc(s_x, 16)
            sp.dma_start(W1s[:, :, :], W1.rearrange("(k p) n -> p k n", p=P)).then_inc(s_w, 16)
            sp.dma_start(b1s[:, :], b1).then_inc(s_w, 16)
            sp.dma_start(W2s[:, :, :], W2.rearrange("(k p) n -> p k n", p=P)).then_inc(s_w, 16)
            sp.dma_start(b2s[:, :], b2.rearrange("(a n) -> a n", a=1).to_broadcast([P, K0])).then_inc(s_w, 16)
            sp.dma_start(VTs[:, :, :], VT.rearrange("(k p) n -> p k n", p=P)).then_inc(s_w, 16)
            sp.dma_start(xT_g[:, :, :], xT[:, 0:GT].rearrange("(k p) n -> p k n", p=P)).then_inc(s_xT, 16)
            sp.dma_start(UTs[:, :, :], UT.rearrange("(k p) n -> p k n", p=P)).then_inc(s_w, 16)
            sp.dma_start(cbs[:, :], cb).then_inc(s_w, 16)
            sp.dma_start(gTs[:, :, :], gT.rearrange("(k p) n -> p k n", p=P)).then_inc(s_w, 16)

            def cond_weights(n, slot):
                which = sp.value_load(i_b1[0:1, bass.ds(n, 1)], min_val=0, max_val=NS1 - 1)
                sp.dma_start(cw_s[:, slot, :, :], cW[bass.ds(which, 1), :, :].rearrange("a (k p) n -> p (a k) n", p=P))\
                  .then_inc(s_cw[slot], 16)

            sp.wait_ge(s_ids, 48)
            for n in range(NW):
                cond_weights(n, n)
            sp.dma_start(sgus[:, :, :, :], sgu.rearrange("(k p) a n -> p k a n", p=P)).then_inc(s_ws, 16)
            for c, (lo, n) in enumerate(SCH):
                sp.dma_start(sds[0:n, c, :], sd[lo:lo + n, :]).then_inc(s_ws, 16)
            sp.wait_ge(s_const, 4)
            sp.dma_start(table.rearrange("(p n) c -> p (n c)", p=P), linit[:, :, :].rearrange("p n c -> p (n c)")).then_inc(s_init, 16)
            sp.dma_start(rows[N:N + P, :], zrow[:, :]).then_inc(s_init, 16)

            def group(g, last):
                if not last:
                    sp.wait_ge(s_mix, 2 * g + 2)
                    sp.sem_inc(s_tick, 1)
                    sp.dma_start(x_g[:, :, :], x[bass.ds((g + 1) * GT, GT), :].rearrange("(t p) d -> p t d", p=P)).then_inc(s_x, 16)
                    sp.wait_ge(s_x1, 2 * g + 2)
                    sp.sem_inc(s_tick, 1)
                    sp.dma_start(xT_g[:, :, :], xT[:, bass.ds((g + 1) * GT, GT)].rearrange("(k p) n -> p k n", p=P)).then_inc(s_xT, 16)
                for m in range(BG - NW if last else BG):
                    sp.wait_ge(s_cwf, g * BG + m + 1)
                    sp.sem_inc(s_tick, 1)
                    cond_weights(g * BG + m + NW, m % NW)
                sp.wait_ge(s_ct, 2 * g + 2)
                sp.sem_inc(s_tick, 1)
                sp.dma_start(rows[bass.ds(g * GT, GT), :].rearrange("(t p) d -> p t d", p=P), ctok[:, :, :]).then_inc(s_rows, 16)

            with sp.Fori(0, G - 1) as g:
                group(g, False)
            group(G - 1, True)

            def weights(e, b):
                sp.dma_start(wb[b], wblk[bass.ds(e, 1), :, :].rearrange("a p n -> p (a n)")).then_inc(s_wb[b], 16)
                sp.dma_start(wt[b], wdt[bass.ds(e, 1), :, :].rearrange("a p n -> p (a n)")).then_inc(s_wb[b], 16)

            weights(0, 0)
            weights(1, 1)
            sp.wait_ge(s_scat, 16 * TOPK * TT)
            sp.dma_start(lst[:, 0:E * TJ, :].rearrange("p n c -> p (n c)"), table.rearrange("(p n) c -> p (n c)", p=P)).then_inc(s_lst, 16)
            weights(2, 2)
            weights(3, 3)
            with sp.Fori(0, E // UE - 1) as i:
                for u in range(UE):
                    sp.wait_ge(s_dp, 2 * (UE * i + u + 1))
                    sp.sem_inc(s_tick, 1)
                    weights(UE * i + u + UE, u)
            for q in range(G):
                if q == 0:
                    sp.wait_ge(s_land, E + 2)
                if q >= 2:
                    sp.wait_ge(s_fin, q - 1)
                for j in range(TJ):
                    sp.dma_start(yin[q % 2][:, j, :, :], acc[j][q * GT:(q + 1) * GT, :].rearrange("(t p) d -> p t d", p=P)).then_inc(s_yin[q % 2], 16)
                if q >= 1:
                    sp.wait_ge(s_fin, q)
                    sp.dma_start(out[(q - 1) * GT:q * GT, :].rearrange("(t p) d -> p t d", p=P), base[:, (q - 1) * TG:q * TG, :]).then_inc(s_out, 16)
            sp.wait_ge(s_fin, G)
            sp.dma_start(out[(G - 1) * GT:G * GT, :].rearrange("(t p) d -> p t d", p=P), base[:, (G - 1) * TG:G * TG, :]).then_inc(s_out, 16)
            sp.wait_ge(s_out, 16 * G)

        @block.gpsimd
        def _(pool):
            pool.sem_inc(s_pf, 1)
            pool.sem_inc(s_land, 1)
            pool.memset(zrow[:, :], 0.0)
            pool.memset(linit[:, :, :], 0)
            pool.memset(ident[:, :], 0.0)
            pool.memset(tri[:, :], 1.0)
            pool.memset(sel[:, :], 1.0)
            pool.memset(onesb[:, :], 1.0)
            pool.memset(ones8[:, :], 1.0)
            pool.iota(e_off_i[:, :], [[TJ, E]], base=0, channel_multiplier=0)
            pool.iota(iota_i[:, :], [[1, E]], base=0, channel_multiplier=0)
            pool.memset(onesf[:, :], 1.0)
            pool.iota(turns_i[:, :], [[16, E // UE], [0, UE]], base=16, channel_multiplier=0)
            pool.iota(pcol_i[:, :], [[0, 1]], base=0, channel_multiplier=1)
            pool.iota(tokid[:, :], [[P, TT]], base=0, channel_multiplier=1).then_inc(s_const, 1)
            pool.wait_ge(s_const, 1)
            pool.affine_select(out=ident[:, :], in_=ident[:, :], compare_op=ALU.not_equal, fill=1.0, base=0,
                               pattern=[[-1, P]], channel_multiplier=1)
            pool.affine_select(out=tri[:, :], in_=tri[:, :], compare_op=ALU.is_gt, fill=0.0, base=0,
                               pattern=[[1, P]], channel_multiplier=-1).then_inc(s_const, 1)
            selv = sel[:, :].rearrange("p (k r) -> p k r", r=R0)
            pool.affine_select(out=selv, in_=selv, compare_op=ALU.is_ge, fill=0.0, base=0,
                               pattern=[[-3, K0], [0, R0]], channel_multiplier=1)
            pool.iota(linit[:, :, 0], [[0, E * TJ]], base=N, channel_multiplier=1).then_inc(s_const, 1)
            pool.wait_ge(s_const, 3)
            pool.affine_select(out=selv, in_=selv, compare_op=ALU.is_ge, fill=0.0, base=2,
                               pattern=[[3, K0], [0, R0]], channel_multiplier=-1)
            pool.tensor_copy(identb[:, :], ident[:, :]).then_inc(s_const, 1)

            for j in range(TJ):
                pool.dma_start(acc[j].rearrange("(p r) d -> p r d", p=P),
                               zrow[:, :].unsqueeze(1).to_broadcast([P, (N + P) // P, D])).then_inc(s_acc if j else s_acc0, 16)
            pool.wait_ge(s_init, 32)
            with pool.Fori(0, G) as g:
                pool.wait_ge(s_pair, g + 1)
                pool.sem_inc(s_tick, 1)
                for t in range(TG):
                    for k in range(TOPK):
                        pool.indirect_dma_start(table, bass.IndirectOffsetOnAxis(sli[:, k, t:t + 1], 0),
                                                pair[:, t, k, :], None, bounds_check=LROWS - 1, oob_is_err=False)\
                            .then_inc(s_scat, 16)
                pool.wait_ge(s_scat, (g + 1) * 16 * TOPK * TG)
                pool.sem_inc(s_pf, 1)

            def gathers(e, u):
                size = get(SIZE, e, u)
                pool.wait_ge(s_gid, e + 1)
                pool.sem_inc(s_tick, 1)

                def gather(j):
                    pool.indirect_dma_start(xg[:, u % UE, j, :], None, rows,
                                            bass.IndirectOffsetOnAxis(gids[:, u % UE, j:j + 1], 0)).then_inc(s_xg[u % UE], 16)

                gather(0)
                with pool.If(size > 0):
                    gather(1)
                    with pool.If(size > 2):
                        gather(2)

            def scatters(e, u):

                def scatter(j):
                    pool.indirect_dma_start(acc[j], bass.IndirectOffsetOnAxis(sids[:, u % UE, j:j + 1], 0),
                                            yo[:, u % 2, j, :], None, compute_op=ALU.add).then_inc(s_acc if j else s_acc0, 16)

                size, landed = get(SIZE, e, u), get(LANDED, e, u)
                pool.wait_ge(s_acc0, 16 * e + 16)
                pool.wait_ge(s_ys, 2 * e + 2)
                pool.sem_inc(s_tick, 1)
                scatter(0)
                pool.wait_ge(s_acc, landed)
                pool.sem_inc(s_land, 1)
                pool.wait_ge(s_ys, 2 * e + 3)
                pool.wait_ge(s_yv, e + 2)
                pool.sem_inc(s_tick, 1)
                with pool.If(size > 0):
                    scatter(1)
                    with pool.If(size > 2):
                        scatter(2)

            pool.wait_ge(s_flags, 1)
            pool.wait_ge(s_lst, 16)
            pool.wait_ge(s_rows, 16 * G)
            pool.sem_inc(s_tick, 1)
            get, start = notes(pool)
            gathers(0, 0)
            gathers(1, 1)
            gathers(2, 2)

            def step(e, u, first=False):
                start(e, u)
                if not (isinstance(e, int) and e >= E - 3):
                    pool.wait_ge(s_xp, 2 * e + (2 if first else 0))
                    pool.sem_inc(s_tick, 1)
                    gathers(e + 3, u + 3)
                if not first:
                    scatters(e - 1, u - 1)

            all_steps(pool, step)
            scatters(E - 1, E - 1)
            landed = pool.value_load(last_wait[0:1, 0:1], min_val=1, max_val=16 * (TJ * E + TJ))
            pool.wait_ge(s_acc0, 16 * E + 16)
            pool.wait_ge(s_acc, landed)
            pool.sem_inc(s_land, 1)

        @block.scalar
        def _(act):
            act.sem_inc(s_ys, 1)
            act.wait_ge(s_cbp, 1)
            act.activation(cbT[:, :, :].rearrange("p k b -> p (k b)"), bank[7][:, 0:DC * B], ACT.Copy).then_inc(s_cbT, 1)
            with act.Fori(0, G) as g:
                act.wait_ge(s_mix, 2 * g + 1)
                act.activation(h0T[:, 0, :], bank[0][:, :], ACT.Copy).then_inc(s_h0, 1)
                for c in range(DC):
                    act.wait_ge(s_hp, 2 * g + 1 + c)
                    act.activation(hT[:, c, :], bank[2 + c][:, :], ACT.Relu, bias=b1s[:, c:c + 1]).then_inc(s_h, 1)
                act.wait_ge(s_e, g + 1)
                act.activation(alp[:, :, :], lg[:, :, :], ACT.Exp).then_inc(s_eo, 1)
                act.wait_ge(s_aTp, g + 1)
                act.activation(alT[:, :], bankb[0:3 * K0, 0:GT], ACT.Copy).then_inc(s_aT, 1)
                for c in range(KC):
                    act.wait_ge(s_sp, KC * g + c + 1)
                    if c >= 2:
                        act.wait_ge(s_z, KC * g + c - 1)
                    act.activation(spread[:, c % 2, :], bank[2 + c % 2][:, :], ACT.Copy).then_inc(s_spr, 1)
                for h in range(2):
                    act.wait_ge(s_x1p, 2 * g + h + 1)
                    act.activation(base[:, bass.ds(g * TG + 2 * h, 2), :],
                                   bank[4 + h][:, :].rearrange("p (t d) -> p t d", d=D), ACT.Copy).then_inc(s_base, 1)
                act.wait_ge(s_c, 2 * g + 2)
                act.activation(cT_all[:, :, bass.ds(g * GT, GT)], cT[:, :, :], ACT.Copy).then_inc(s_call, 1)
                for h in range(2):
                    act.wait_ge(s_ctp, 2 * g + h + 1)
                    act.activation(ctok[:, 2 * h:2 * h + 2, :].rearrange("p t d -> p (t d)"), bank[h][:, :], ACT.Copy).then_inc(s_ct, 1)
                act.wait_ge(s_m8, g + 1)
                act.activation(Lm[:, :, :], Lm[:, :, :], ACT.Exp).then_inc(s_m8e, 1)
                act.activation(v8m[:, :, :], v8m[:, :, :], ACT.Exp).then_inc(s_m8e, 1)
                act.wait_ge(s_rows, 16 * g + 16)
            with act.Fori(0, G) as g:
                for c, (lo, n) in enumerate(SCH):
                    act.wait_ge(s_sh, len(SCH) * g + c + 1)
                    act.activation(sil[0:n, c, :], bank[2 * c][0:n, :], ACT.Silu).then_inc(s_sil, 1)

            def tokens(e, u):
                act.wait_ge(s_xp, 2 * e + 1)
                act.activation(xgT[:, u % 2, 0, :], bank[0][:, 0:CAP], ACT.Copy).then_inc(s_xs, 1)

            def step(e, u, first=False):
                act.wait_ge(s_gu, 3 * e + 1)
                act.activation(sg[:, 0, :], bank[2][:, 0:CAP], ACT.Silu).then_inc(s_sg, 1)
                act.wait_ge(s_gu, 3 * e + 3)
                act.activation(sg[0:FT, 1, :], bank[4][0:FT, 0:CAP], ACT.Silu).then_inc(s_sg, 1)
                if not (isinstance(e, int) and e == E - 1):
                    tokens(e + 1, u + 1)
                if not first:
                    rows_out(e - 1, u - 1)

            def rows_out(e, u):
                act.wait_ge(s_ids2, 2 * e + 2)
                act.wait_ge(s_land, e + 1)
                for j in range(2):
                    act.wait_ge(s_dp, 2 * e + 1 + j)
                    act.activation(yo[:, u % 2, j, :], bank[5 + j][:, 0:D], ACT.Copy, scale=wcol[:, u % UE, j:j + 1]).then_inc(s_ys, 1)

            tokens(0, 0)
            all_steps(act, step)
            rows_out(E - 1, E - 1)

        @block.vector
        def _(dve):
            v = nc.vector
            done = [0, 0]

            def link(ins, g=0):
                done[1] += 1
                ins.then_inc(s_v, 1)
                dve.wait_ge(s_v, g * PV + (done[0] + done[1]))

            dve.sem_inc(s_yv, 1)
            v.memset(mc[:, :, :], 0.0)
            v.memset(gath0[:, :, :], 0.0)
            v.memset(hh[:, :, :, :], 0.0)
            v.memset(lst[:, E * TJ:, :], 0)
            v.memset(bd[:, :, :], 0.0)
            dve.wait_ge(s_const, 1)
            v.tensor_copy(iota64[:, :], iota_i[:, :])
            v.tensor_copy(e_off[:, :], e_off_i[:, :])
            v.tensor_copy(turns[:, :], turns_i[:, :])
            link(v.tensor_copy(pcol[:, :], pcol_i[:, :]))
            dve.wait_ge(s_ids, 48)
            v.tensor_copy(f_q0[:, :], i_q0[:, :])
            v.tensor_copy(f_b0[:, :], i_b0[:, :])
            link(v.tensor_copy(f_b1[:, :], i_b1[:, :]))
            v.tensor_scalar(oh1[:, :], f_b1[:, :], pcol[0:NS1, 0:1], None, ALU.is_equal).then_inc(s_dve0, 1)
            link(v.tensor_scalar(f_b0[:, :], f_b0[:, :], pcol[0:NS0, 0:1], None, ALU.is_equal))
            dve.wait_ge(s_wall, 16 * (BT + 1))
            v.tensor_tensor(bias0[:, :, :], f_b0[:, :].unsqueeze(2).to_broadcast([NS0, B, S]),
                            fs_s[:, :].unsqueeze(1).to_broadcast([NS0, B, S]), ALU.mult)
            for n in range(NS0):
                last = v.tensor_scalar(maskq[:, n, :], f_q0[:, :], float(n), None, ALU.is_equal)
            link(last)
            for n in range(NS0):
                link(v.copy_predicated(gath0[:, :, :], maskq[:, n, :].unsqueeze(2).to_broadcast([P, TT, S]),
                                       wall[:, n, :].unsqueeze(1).to_broadcast([P, TT, S])))
            for q in range(BT):
                last = v.tensor_copy(bd[q * S:(q + 1) * S, :, q * S:(q + 1) * S], gath0[q * S:(q + 1) * S, :, :])
            last.then_inc(s_dve0, 1)
            done[0], done[1] = done[1], 0

            with dve.Fori(0, G) as g:
                done[1] = 0
                dve.wait_ge(s_mix, 2 * g + 2)
                v.tensor_copy(h0T[:, 1, :], bank[1][:, :]).then_inc(s_h0, 1)
                dve.wait_ge(s_lp, g + 1)
                link(v.tensor_tensor(lg[:, :, :], bank[0][:, 0:TG * K0].rearrange("p (t k) -> p t k", k=K0),
                                     b2s[:, :].unsqueeze(1).to_broadcast([P, TG, K0]), ALU.add), g)
                link(v.reduce_max(lgm[:, :], lg[:, :, :], AX.X), g)
                v.tensor_tensor(lg[:, :, :], lg[:, :, :], lgm[:, :].unsqueeze(2).to_broadcast([P, TG, K0]),
                                ALU.subtract).then_inc(s_e, 1)
                dve.wait_ge(s_eo, g + 1)
                link(v.reduce_sum(lgm[:, :], alp[:, :, :], AX.X), g)
                link(v.reciprocal(lgm[:, :], lgm[:, :]), g)
                link(v.tensor_tensor(alp[:, :, :], alp[:, :, :], lgm[:, :].unsqueeze(2).to_broadcast([P, TG, K0]), ALU.mult), g)
                link(v.tensor_copy(als[:, :, :, 0], alp[:, :, :]), g)
                link(v.tensor_tensor(alr[:, :, :], alp[:, :, :], als[:, :, :, 0], ALU.subtract), g)
                link(v.tensor_copy(als[:, :, :, 1], alr[:, :, :]), g)
                link(v.tensor_tensor(alr[:, :, :], alr[:, :, :], als[:, :, :, 1], ALU.subtract), g)
                v.tensor_copy(als[:, :, :, 2], alr[:, :, :]).then_inc(s_al, 1)
                for c in range(KC):
                    dve.wait_ge(s_vx, KC * g + c + 1)
                    dve.wait_ge(s_spr, KC * g + c + 1)
                    v.tensor_tensor(z[:, c, :], spread[:, c % 2, :], bank[4 + c][:, :], ALU.mult).then_inc(s_z, 1)
                dve.wait_ge(s_xT, 16 * g + 16)
                for c in range(DC):
                    dve.wait_ge(s_up, DC * g + c + 1)
                    v.tensor_tensor(x1T[:, c, :], xT_g[:, c, :], bank[c][:, :], ALU.add).then_inc(s_x1, 1)
                dve.wait_ge(s_cbT, 1)
                dve.wait_ge(s_cwf, BG * g + BG)
                for c in range(DC):
                    v.tensor_tensor(cT[:, c, :].rearrange("p (b s) -> p b s", s=S),
                                    bank[6 + c][:, :].rearrange("p (b s) -> p b s", s=S),
                                    cbT[:, c, bass.ds(g * BG, BG)].unsqueeze(2).to_broadcast([P, BG, S]), ALU.add).then_inc(s_c, 1)
                dve.wait_ge(s_rp, g + 1)
                link(v.tensor_copy(Ls[:, :, :].rearrange("p t e -> p (t e)"), bank[2][:, 0:TG * E]), g)
                dve.sem_inc(s_tick, 1)
                for t in range(TG):
                    last = v.max(v8[:, t, :], Ls[:, t, :])
                link(last, g)
                v.tensor_tensor(Lm[:, :, :], Ls[:, :, :], v8[:, :, 0:1].to_broadcast([P, TG, E]), ALU.subtract)
                v.tensor_tensor(v8m[:, :, :], v8[:, :, :], v8[:, :, 0:1].to_broadcast([P, TG, 8]), ALU.subtract).then_inc(s_m8, 1)
                for t in range(TG):
                    last = v.max_index(i8[:, t, :], v8[:, t, :], Ls[:, t, :])
                link(last, g)
                v.tensor_copy(mc[:, 0, :], mc[:, TG, :])
                link(v.tensor_copy(i8f[:, :, :], i8[:, :, :]), g)
                for k in range(TOPK):
                    last = v.tensor_tensor(OH[:, k, :].rearrange("p (t e) -> p t e", e=E),
                                           iota64[:, :].unsqueeze(1).to_broadcast([P, TG, E]),
                                           i8f[:, :, k:k + 1].to_broadcast([P, TG, E]), ALU.is_equal)
                link(last, g)
                with nc.allow_low_precision(reason="counts up to 16 are exact"):
                    link(v.reduce_sum(M[:, :], OH[:, :, :].rearrange("p k n -> p n k"), AX.X), g)
                    for t in range(TG):
                        last = v.tensor_tensor(mc[:, t + 1, :], mc[:, t, :], M[:, t * E:(t + 1) * E], ALU.add)
                        if t < TG - 1:
                            link(last, g)
                last.then_inc(s_M, 1)
                dve.wait_ge(s_m8e, 2 * g + 2)
                link(v.reduce_sum(zs[:, :], Lm[:, :, :], AX.X), g)
                link(v.reciprocal(zs[:, :], zs[:, :]), g)
                link(v.tensor_tensor(v8m[:, :, :], v8m[:, :, :], zs[:, :].unsqueeze(2).to_broadcast([P, TG, 8]), ALU.mult), g)
                link(v.reduce_sum(s6[:, :], v8m[:, :, 0:TOPK], AX.X), g)
                link(v.tensor_scalar(s6[:, :], s6[:, :], 1e-20, None, ALU.add), g)
                link(v.reciprocal(s6[:, :], s6[:, :]), g)
                dve.wait_ge(s_pf, g + 1)
                v.tensor_tensor(pair[:, :, :, 1].bitcast(F32), v8m[:, :, 0:TOPK],
                                s6[:, :].unsqueeze(2).to_broadcast([P, TG, TOPK]), ALU.mult)
                v.tensor_copy(pair[:, :, :, 0], tokid[:, bass.ds(g * TG, TG)].unsqueeze(2).to_broadcast([P, TG, TOPK]))
                dve.wait_ge(s_rk, g + 1)
                v.tensor_scalar(sa[:, :], bank[3][:, 0:TG * E], float(P), float(1 - LROWS), ALU.is_ge, ALU.mult)
                v.tensor_scalar(sbb[:, :], bank[3][:, 0:TG * E], float(2 * P), float(1 - LROWS), ALU.is_ge, ALU.mult)
                v.scalar_tensor_tensor(sc[:, :].rearrange("p (t e) -> p t e", e=E), bank[3][:, 0:TG * E].rearrange("p (t e) -> p t e", e=E),
                                       float(E * TJ), e_off[:, :].unsqueeze(1).to_broadcast([P, TG, E]), ALU.mult, ALU.add).then_inc(s_rkr, 1)
                dve.wait_ge(s_rkr, g + 1)
                link(v.tensor_tensor(sa[:, :], sa[:, :], sbb[:, :], ALU.add), g)
                link(v.tensor_tensor(sc[:, :], sc[:, :], sa[:, :], ALU.add), g)
                link(v.tensor_tensor(OH[:, :, :], OH[:, :, :], sc[:, :].unsqueeze(1).to_broadcast([P, TOPK, TG * E]), ALU.mult), g)
                link(v.reduce_sum(slf[:, :, :], OH[:, :, :].rearrange("p k (t e) -> p k t e", e=E), AX.X), g)
                v.tensor_copy(sli[:, :, :], slf[:, :, :]).then_inc(s_pair, 1)
                assert done[1] == PV, done

            steps = [0]

            def flink(ins):
                steps[0] += 1
                ins.then_inc(s_fl, 1)
                dve.wait_ge(s_fl, steps[0])

            dve.wait_ge(s_cnt, 1)
            for i, n in enumerate(SIZES[:-1]):
                last = v.tensor_scalar(more[:, i, :], bank[7][:, 0:E], n + 0.5, None, ALU.is_ge)
            flink(last)
            with nc.allow_low_precision(reason="counts up to 4 are exact"):
                v.reduce_sum(facts[:, SIZE, :], more[:, :, :].rearrange("p i e -> p e i"), AX.X)
            flink(v.tensor_tensor(tiles_f[:, :], more[:, SIZES.index(P), :], more[:, SIZES.index(2 * P), :], ALU.add))
            flink(v.tensor_tensor_scan(seen[:, :], onesf[:, :], tiles_f[:, :], 0.0, ALU.mult, ALU.add))
            flink(v.tensor_tensor(fl[:, :], seen[:, :], tiles_f[:, :], ALU.subtract))
            v.tensor_scalar(facts[:, LANDED, :], fl[:, :], 16.0, 16.0 * (TJ - 1), ALU.mult, ALU.add)
            flink(v.tensor_scalar(last_wait[:, :], seen[:, E - 1:E], 16.0, 16.0 * (TJ - 1), ALU.mult, ALU.add))
            for u in range(UE):
                last = v.tensor_tensor_scan(seen[:, u:E:UE], onesf[:, 0:E:UE], tiles_f[:, u:E:UE], 0.0, ALU.mult, ALU.add)
            flink(last)
            v.scalar_tensor_tensor(facts[:, GATHERED, :], seen[:, :], 16.0, turns[:, :], ALU.mult, ALU.add).then_inc(s_flags, 1)

            dve.wait_ge(s_base, 2 * G)
            with dve.Fori(0, G) as g:
                for c, (lo, n) in enumerate(SCH):
                    dve.wait_ge(s_sil, len(SCH) * g + c + 1)
                    v.tensor_tensor(hs[0:n, c, :], sil[0:n, c, :], bank[2 * c + 1][0:n, :], ALU.mult).then_inc(s_hs, 1)
                for h in range(2):
                    dve.wait_ge(s_sdp, 2 * g + h + 1)
                    rows2 = base[:, bass.ds(g * TG + 2 * h, 2), :]
                    v.tensor_tensor(rows2, rows2, bank[6 + h][:, :].rearrange("p (t d) -> p t d", d=D), ALU.add).then_inc(s_sb, 1)

            def tokens(e, u):
                dve.wait_ge(s_xp, 2 * e + 2)
                v.tensor_copy(xgT[:, u % 2, 1, :], bank[1][:, 0:CAP]).then_inc(s_xv, 1)

            def gather_ids(e, u):
                v.tensor_copy(gids[:, u % UE, :], lst[:, bass.ds(e * TJ, TJ), 0]).then_inc(s_gid, 1)

            def slots(e, u):
                v.tensor_copy(sids[:, u % UE, :], lst[:, bass.ds(e * TJ, TJ), 0]).then_inc(s_ids2, 1)
                v.tensor_copy(wcol[:, u % UE, :], lst[:, bass.ds(e * TJ, TJ), 1].bitcast(F32)).then_inc(s_ids2, 1)

            def rows_out(e, u):
                dve.wait_ge(s_ids2, 2 * e + 2)
                dve.wait_ge(s_land, e + 1)
                dve.wait_ge(s_dp, 2 * e + 2)
                v.tensor_scalar(yo[:, u % 2, 2, :], bank[7][:, 0:D], wcol[:, u % UE, 2:3], None, ALU.mult).then_inc(s_yv, 1)

            def step(e, u, first=False):
                dve.wait_ge(s_sg, 2 * e + 1)
                dve.wait_ge(s_gu, 3 * e + 2)
                v.tensor_tensor(hh[:, u % 2, 0, :], sg[:, 0, :], bank[3][:, 0:CAP], ALU.mult).then_inc(s_hh, 1)
                dve.wait_ge(s_sg, 2 * e + 2)
                v.tensor_tensor(hh[0:FT, u % 2, 1, :], sg[0:FT, 1, :], bank[4][CU:CU + FT, 0:CAP], ALU.mult).then_inc(s_hh, 1)
                if not (isinstance(e, int) and e == E - 1):
                    tokens(e + 1, u + 1)
                if not first:
                    rows_out(e - 1, u - 1)
                slots(e, u)
                if not (isinstance(e, int) and e >= E - 4):
                    gather_ids(e + 4, u + 4)

            dve.wait_ge(s_lst, 16)
            for e in range(4):
                gather_ids(e, e)
            tokens(0, 0)
            all_steps(dve, step)
            rows_out(E - 1, E - 1)

            for q in range(G):
                dve.wait_ge(s_yin[q % 2], 16 * TJ * (q // 2 + 1))
                part = base[:, q * TG:(q + 1) * TG, :]
                for j in range(TJ):
                    last = v.tensor_tensor(part, part, yin[q % 2][:, j, :, :], ALU.add)
                    if j < TJ - 1:
                        last.then_inc(s_cv, 1)
                        dve.wait_ge(s_cv, q * (TJ - 1) + j + 1)
                last.then_inc(s_fin, 1)

        @block.tensor
        def _(pe):
            mm, tr = nc.tensor.matmul, nc.tensor.transpose
            pe.wait_ge(s_w, 16 * 8)
            pe.wait_ge(s_dve0, 2)
            pe.wait_ge(s_const, 4)
            for c in range(DC):
                last = mm(bank[7][:, c * B:(c + 1) * B], cbs[:, c * P:(c + 1) * P], oh1[:, :], start=True, stop=True)
            last.then_inc(s_cbp, 1)
            pe.wait_ge(s_cbT, 1)
            with pe.Fori(0, G) as g:
                pe.wait_ge(s_x, 16 * g + 16)
                for c in range(DC):
                    for t in range(TG):
                        o = bank[c][:, t * P:(t + 1) * P]
                        mm(o, x_g[:, t, c * P:(c + 1) * P], bd[:, bass.ds(g * TG + t, 1), :].rearrange("p a n -> p (a n)"),
                           start=True, stop=False)
                        last = mm(o, ones8[:, :], bias0[:, bass.ds((g * TG + t) * BT, BT), :].rearrange("p b s -> p (b s)"),
                                  start=False, stop=True)
                    last.then_inc(s_mix, 1)
                pe.wait_ge(s_h0, 2 * g + 2)
                for o in range(DC):
                    for c in range(DC):
                        last = mm(bank[2 + o][:, :], W1s[:, c, o * P:(o + 1) * P], h0T[:, c, :], start=c == 0, stop=c == DC - 1)
                    last.then_inc(s_hp, 1)

                def vx(o):
                    for c in range(DC):
                        last = mm(bank[4 + o][:, :], VTs[:, c, o * P:(o + 1) * P], h0T[:, c, :], start=c == 0, stop=c == DC - 1)
                    last.then_inc(s_vx, 1)

                vx(0)
                pe.wait_ge(s_h, 2 * g + 2)
                for t in range(TG):
                    for c in range(DC):
                        last = mm(bank[0][:, t * K0:(t + 1) * K0], hT[:, c, t * P:(t + 1) * P], W2s[:, c, :],
                                  start=c == 0, stop=c == DC - 1)
                last.then_inc(s_lp, 1)
                for o in range(1, KC):
                    vx(o)
                pe.wait_ge(s_al, g + 1)
                for t in range(TG):
                    last = tr(bankb[0:3 * K0, t * P:(t + 1) * P], als[:, t, :, :].rearrange("p k a -> p (k a)"), identb[:, :])
                last.then_inc(s_aTp, 1)
                pe.wait_ge(s_aT, g + 1)
                for c in range(KC):
                    if c >= 2:
                        pe.wait_ge(s_spr, KC * g + c - 1)
                    mm(bank[2 + c % 2][:, :], sel[:, c * P:(c + 1) * P], alT[:, :], start=True, stop=True).then_inc(s_sp, 1)
                pe.wait_ge(s_z, KC * g + KC)
                for o in range(DC):
                    for c in range(KC):
                        last = mm(bank[o][:, :], UTs[:, c, o * P:(o + 1) * P], z[:, c, :], start=c == 0, stop=c == KC - 1)
                    last.then_inc(s_up, 1)
                pe.wait_ge(s_x1, 2 * g + 2)
                for t in range(TG):
                    for c in range(DC):
                        last = tr(bank[4 + t // 2][:, (t % 2) * D + c * P:(t % 2) * D + (c + 1) * P], x1T[:, c, t * P:(t + 1) * P], ident[:, :])
                    if t % 2:
                        last.then_inc(s_x1p, 1)
                for m in range(BG):
                    pe.wait_ge(s_cw[m % NW], 16 * (BG // NW * g + m // NW + 1))
                    for o in range(DC):
                        for c in range(DC):
                            last = mm(bank[6 + o][:, m * S:(m + 1) * S], cw_s[:, m % NW, c, o * P:(o + 1) * P],
                                      x1T[:, c, m * S:(m + 1) * S], start=c == 0, stop=c == DC - 1)
                    last.then_inc(s_cwf, 1)
                pe.wait_ge(s_c, 2 * g + 2)
                for t in range(TG):
                    for c in range(DC):
                        last = mm(bank[2][:, t * E:(t + 1) * E], cT[:, c, t * P:(t + 1) * P], gTs[:, c, :], start=c == 0, stop=c == DC - 1)
                last.then_inc(s_rp, 1)
                for t in range(TG):
                    for c in range(DC):
                        last = tr(bank[t // 2][:, (t % 2) * D + c * P:(t % 2) * D + (c + 1) * P], cT[:, c, t * P:(t + 1) * P], ident[:, :])
                    if t % 2:
                        last.then_inc(s_ctp, 1)
                pe.wait_ge(s_M, g + 1)
                for t in range(TG):
                    mm(bank[3][:, t * E:(t + 1) * E], tri[:, :], M[:, t * E:(t + 1) * E], start=True, stop=False)
                    last = mm(bank[3][:, t * E:(t + 1) * E], onesb[:, :], mc[:, t, :], start=False, stop=True)
                last.then_inc(s_rk, 1)
                pe.wait_ge(s_ct, 2 * g + 2)
                pe.wait_ge(s_rkr, g + 1)
            mm(bank[7][:, 0:E], onesb[:, :], mc[:, TG, :], start=True, stop=True).then_inc(s_cnt, 1)
            pe.wait_ge(s_ws, 16 * (1 + len(SCH)))
            pe.wait_ge(s_call, G)
            with pe.Fori(0, G) as g:
                for s_, (lo, n) in enumerate(SCH):
                    for a in range(2):
                        for c in range(DC):
                            last = mm(bank[2 * s_ + a][0:n, :], sgus[:, c, a, lo:lo + n], cT_all[:, c, bass.ds(g * GT, GT)],
                                      start=c == 0, stop=c == DC - 1)
                    last.then_inc(s_sh, 1)
                pe.wait_ge(s_hs, len(SCH) * (g + 1))
                for t in range(TG):
                    for s_, (lo, n) in enumerate(SCH):
                        last = mm(bank[6 + t // 2][:, (t % 2) * D:(t % 2 + 1) * D], hs[0:n, s_, t * P:(t + 1) * P], sds[0:n, s_, :],
                                  start=s_ == 0, stop=s_ == len(SCH) - 1)
                    if t % 2:
                        last.then_inc(s_sdp, 1)
                pe.wait_ge(s_sb, 2 * g + 2)

            get, start = notes(pe)

            def tokens(e, u):
                def work(tiles):
                    pe.wait_ge(s_xg[u % UE], gathered)
                    for c in range(DC):
                        for j in range(tiles):
                            last = tr(bank[c][:, j * P:(j + 1) * P], xg[:, u % UE, j, c * P:(c + 1) * P], ident[:, :])
                        last.then_inc(s_xp, 1)

                gathered = get(GATHERED, e, u)
                by_tiles(pe, get(SIZE, e, u), work)

            def step(e, u, first=False):
                b = u % UE

                def gate_up(n):
                    pe.wait_ge(s_wb[b], (32 // UE) * (e - b + UE))
                    pe.wait_ge(s_xs, e + 1)
                    pe.wait_ge(s_xv, e + 1)
                    if not first:
                        pe.wait_ge(s_hh, 2 * e)
                    for o, w, m in ((2, g_first, FR), (3, u_first, FR), (4, rest, CU + FT)):
                        for c in range(DC):
                            ins = mm(bank[o][0:m, 0:n], w(b, c), xgT[:, u % 2, c, 0:n], start=c == 0, stop=c == DC - 1)
                        ins.then_inc(s_gu, 1)

                start(e, u)
                by_rows(get(SIZE, e, u), gate_up)
                if not (isinstance(e, int) and e == E - 1):
                    tokens(e + 1, u + 1)
                if not first:
                    down(e - 1, u - 1)

            def down(e, u):
                def work(tiles):
                    pe.wait_ge(s_hh, 2 * e + 2)
                    pe.wait_ge(s_ys, 2 * e + 1)
                    pe.wait_ge(s_yv, e + 1)
                    for j in (0, 2, 1)[:1 if tiles == 1 else 3]:
                        if j < tiles:
                            o = bank[5 + j][:, 0:D]
                            mm(o, hh[:, u % 2, 0, j * P:(j + 1) * P], down_first(u % UE), start=True, stop=False)
                            last = mm(o, hh[0:FT, u % 2, 1, j * P:(j + 1) * P], wt[u % UE], start=False, stop=True)
                        if j != 2:
                            last.then_inc(s_dp, 2 if tiles == 1 else 1)

                by_tiles(pe, get(SIZE, e, u), work)

            def by_rows(size, work):
                with pe.If(size > 1):
                    with pe.If(size > 2):
                        with pe.If(size > 3):
                            work(SIZES[4])
                        with pe.Else():
                            work(SIZES[3])
                    with pe.Else():
                        work(SIZES[2])
                with pe.Else():
                    with pe.If(size > 0):
                        work(SIZES[1])
                    with pe.Else():
                        work(SIZES[0])

            pe.wait_ge(s_flags, 1)
            pe.sem_inc(s_tick, 1)
            tokens(0, 0)
            all_steps(pe, step)
            down(E - 1, E - 1)


IN = ["x", "xT", "idq0", "idb0", "idb1", "w0", "fs0", "W1", "b1", "W2", "b2", "VT", "UT", "cW", "cb", "gT", "wblk", "wdt", "sgu", "sd"]


def kernel(x, itok_B_0_7, fside_8xS_0, itok_B_0_15, L0_cond_weights, L0_ffn_U, L0_ffn_V, L0_ffn_W1, L0_ffn_b1,
           L0_ffn_W2, L0_ffn_b2, L1_cond_W, L1_cond_b, L1_ffn_gate_w, L1_ffn_w_gate, L1_ffn_w_up, L1_ffn_w_down,
           L1_ffn_sh_gate, L1_ffn_sh_up, L1_ffn_sh_down):
    import numpy as np
    import concourse.bacc as bacc
    from concourse.bass_utils import run_bass_kernel_spmd

    x2 = np.asarray(x).reshape(N, D)
    ids0, ids1 = np.asarray(itok_B_0_7), np.asarray(itok_B_0_15)

    def packed(w_gate, w_up, w_down):
        g = np.asarray(w_gate).transpose(0, 2, 1).reshape(E, DC, P, F).transpose(0, 2, 1, 3)
        u = np.asarray(w_up).transpose(0, 2, 1).reshape(E, DC, P, F).transpose(0, 2, 1, 3)
        gap = np.zeros((E, P, DC, CU - FT), g.dtype)
        gu = np.concatenate([g, gap, u[..., FR:], u[..., :FR]], axis=3).reshape(E, P, WROW - D)
        d = np.asarray(w_down).transpose(0, 2, 1)
        return np.concatenate([gu, d[:, :FR]], axis=2), d[:, FR:]

    wblk, wdt = packed(L1_ffn_w_gate, L1_ffn_w_up, L1_ffn_w_down)
    arrays = {
        "x": x2, "xT": x2.T,
        "idq0": np.repeat(ids0.reshape(TT, BT).T, S, axis=0),
        "idb0": np.repeat(ids0.reshape(1, B), NS0, axis=0),
        "idb1": np.repeat(ids1.reshape(1, B), NS1, axis=0),
        "w0": L0_cond_weights, "fs0": fside_8xS_0,
        "W1": L0_ffn_W1, "b1": np.asarray(L0_ffn_b1).reshape(DC, P).T, "W2": L0_ffn_W2, "b2": L0_ffn_b2,
        "VT": np.asarray(L0_ffn_V).reshape(KR, D).T,
        "UT": np.asarray(L0_ffn_U).transpose(0, 2, 1).reshape(KR, D),
        "cW": L1_cond_W, "cb": L1_cond_b, "gT": np.asarray(L1_ffn_gate_w).T,
        "wblk": wblk, "wdt": wdt,
        "sgu": np.stack([np.asarray(L1_ffn_sh_gate).T, np.asarray(L1_ffn_sh_up).T], axis=1),
        "sd": np.asarray(L1_ffn_sh_down).T,
    }
    nc = bacc.Bacc("TRN2", target_bir_lowering=False, num_devices=1)
    aps = []
    for name in IN:
        a = np.ascontiguousarray(arrays[name])
        arrays[name] = a
        aps.append(nc.dram_tensor(f"in_{name}", a.shape, mybir.dt.from_np(a.dtype), kind="ExternalInput").ap())
    out = nc.dram_tensor("out_y", (N, D), F32, kind="ExternalOutput").ap()
    program(nc, *aps, out)
    r = run_bass_kernel_spmd(nc, [{f"in_{k}": a for k, a in arrays.items()}], core_ids=[0])
    return r.results[0]["out_y"].reshape(B, S, D)
```

```python
from contextlib import ExitStack

import concourse.bass as bass
from concourse import mybir

F32 = mybir.dt.float32
BF16 = mybir.dt.bfloat16
I32 = mybir.dt.int32
U32 = mybir.dt.uint32
ALU = mybir.AluOpType
ACT = mybir.ActivationFunctionType
AX = mybir.AxisListType

P = 128
B, S, D = 64, 32, 256
N = B * S
NS0, NS1 = 8, 16
K0, R0 = 8, 64
E, TOPK, F, FS = 64, 6, 176, 352
CAP = 2 * ((N * TOPK + E - 1) // E)
DC = D // P
G = 4
GT = N // G
TG = GT // P
TT = N // P
BG = B // G
BT = P // S
KR = K0 * R0
KC = KR // P
TJ = CAP // P
NROWS = N + TJ * P
LROWS = P * E * TJ
FR, FT = P, F - P
CU = 64
WROW = DC * (FR + CU + FT + FR) + D
SCH = [(0, P), (P, P), (2 * P, FS - 2 * P)]
UE = 4
UL = 16
LOOPS = E // UL - 1
SIZES = [P, 3 * P // 2, 2 * P, 5 * P // 2, CAP]
TWO, THREE = SIZES.index(P), SIZES.index(2 * P)
SIZE, LANDED, GATHERED = range(3)
assert TJ * P == CAP and G * GT == N


def program(nc, x, xT, idq0, idb0, idb1, w0, fs0, W1, b1, W2, b2, VT, UT, cW, cb, gT, wblk, wdt, sgu, sd, out):
    ctx = ExitStack()
    with ctx:
        def sb(name, shape, dt=F32):
            return ctx.enter_context(nc.sbuf_tensor(name, shape, dt))

        def sem(name):
            return ctx.enter_context(nc.semaphore(name))

        rows = nc.dram_tensor("token_rows", [NROWS, D], F32).ap()
        condT_rows = nc.dram_tensor("condT", [G - 1, P, DC * GT], F32).ap()
        table = nc.dram_tensor("slot_table", [LROWS, 2], I32).ap()
        acc = [nc.dram_tensor(f"acc{j}", [NROWS, D], F32).ap() for j in range(2)]

        ident = sb("ident", [P, P])
        identb = sb("identb", [P, P], BF16)
        tri = sb("tri", [P, P], BF16)
        onesb = sb("onesb", [P, P], BF16)
        sel = sb("sel", [3 * K0, KR], BF16)
        iota64 = sb("iota64", [P, E])
        e_off = sb("e_off", [P, E])
        pcol = sb("pcol", [P, 1])
        iota_i = sb("iota_i", [P, E], I32)
        e_off_i = sb("e_off_i", [P, E], I32)
        pcol_i = sb("pcol_i", [P, 1], I32)
        tokid = sb("tokid", [P, TT], I32)
        zrow = sb("zrow", [P, D])
        linit = sb("linit", [P, E * TJ, 2], I32)
        i_q0 = sb("i_q0", [P, TT], I32)
        f_q0 = sb("f_q0", [P, TT])
        i_b0 = sb("i_b0", [NS0, B], I32)
        i_b1 = sb("i_b1", [1, B], I32)
        f_b0 = sb("f_b0", [NS0, B])
        maskq = sb("maskq", [P, NS0, TT], U32)
        mixd = sb("mixd", [P, 5 * N // 2])
        bd = mixd[:, 0:N].rearrange("p (t n) -> p t n", n=P)
        fs_s = sb("fs_s", [NS0, S])
        fs3 = sb("fs3", [NS0, 3, S], BF16)
        fsr = sb("fsr", [NS0, S])
        bias0 = mixd[0:NS0, N:5 * N // 2].bitcast(BF16).rearrange("p (a b s) -> p a b s", a=3, s=S)
        cTs = mixd[:, 0:DC * N].rearrange("p (g k n) -> p g k n", k=DC, n=GT)
        W1s = sb("W1s", [P, DC, D])
        b1s = sb("b1s", [P, DC])
        W2s = sb("W2s", [P, DC, K0])
        b2s = sb("b2s", [P, K0])
        VTs = sb("VTs", [P, DC, KR])
        UTs = sb("UTs", [P, KC, D])
        cbs = sb("cbs", [NS1, D])
        cbr = sb("cbr", [NS1, D])
        cb3 = sb("cb3", [NS1, 3, D], BF16)
        cbk = sb("cbk", [P, NS1, D], BF16)
        cw = sb("cw", [P, NS1, DC, D])
        gTs = sb("gTs", [P, DC, E])
        sgus = sb("sgus", [P, DC, 2, FS])
        sds = sb("sds", [P, len(SCH), D])
        base = sb("base", [P, TT, D])
        x_g = sb("x_g", [P, TG, D])
        xT_g = sb("xT_g", [P, DC, GT])
        h0T = sb("h0T", [P, DC, GT])
        hT = sb("hT", [P, DC, GT])
        lg = sb("lg", [P, TG, K0])
        lgm = sb("lgm", [P, TG])
        alp = sb("alp", [P, TG, K0])
        alr = sb("alr", [P, TG, K0])
        als = sb("als", [P, TG, K0, 3], BF16)
        alT = sb("alT", [3 * K0, GT], BF16)
        spread = sb("spread", [P, 2, GT])
        z = sb("z", [P, KC, GT])
        x1T = sb("x1T", [P, DC, GT])
        cT = sb("cT", [P, DC, GT])
        ctok2 = sb("ctok2", [S, BG // 2, D])
        ctok = [z[0:S, :, :].rearrange("p k n -> p (k n)")[:, 0:BG // 2 * D].rearrange("p (b d) -> p b d", d=D), ctok2[:, :, :]]
        Ls = sb("Ls", [P, TG, E])
        Lm = sb("Lm", [P, TG, E])
        v8 = sb("v8", [P, TG, 8])
        i8 = sb("i8", [P, TG, 8], U32)
        i8f = sb("i8f", [P, TG, 8])
        v8m = sb("v8m", [P, TG, 8])
        zs = sb("zs", [P, TG])
        s6 = sb("s6", [P, TG])
        OH = sb("OH", [P, TOPK, TG * E])
        M = sb("M", [P, TG * E], BF16)
        mc = sb("mc", [P, TG + 1, E], BF16)
        sa = sb("sa", [P, TG * E])
        sbb = sb("sbb", [P, TG * E])
        sc = sb("sc", [P, TG * E])
        slf = sb("slf", [P, TOPK, TG])
        sli = sb("sli", [P, TOPK, TG], I32)
        pair = sb("pair", [P, TG, TOPK, 2], I32)
        sil = sb("sil", [P, len(SCH), GT])
        hs = sb("hs", [P, len(SCH), GT])
        wall = hs[:, 0, 0:NS0 * S].rearrange("p (n s) -> p n s", s=S)
        gath0 = sil[:, 0, 0:TT * S].rearrange("p (t s) -> p t s", s=S)
        lst = sb("lst", [P, E * TJ, 2], I32)
        wb2 = sb("wb2", [P, 2, WROW])
        wt2 = sb("wt2", [FT, 2, D])
        wb = [wb2[:, 0, :], wb2[:, 1, :]] + [t[:, :, :].rearrange("p k n -> p (k n)")[:, 0:WROW] for t in (h0T, hT)]
        wt = [wt2[:, 0, :], wt2[:, 1, :]] + [spread[0:FT, i, 0:D] for i in range(2)]
        facts = sb("facts", [P, 3, E], I32)
        tiles_f = sb("tiles_f", [P, E])
        seen = sb("seen", [P, E])
        fl = sb("fl", [P, E])
        onesf = sb("onesf", [P, E])
        last_wait = sb("last_wait", [P, 2], I32)
        more = sb("more", [P, len(SIZES) - 1, E])
        gids = sb("gids", [P, UE, TJ], I32)
        sids = sb("sids", [P, UE, TJ], I32)
        wcol = sb("wcol", [P, UE, TJ])
        cw_flat = cw[:, :, :, :].rearrange("p s k n -> p (s k n)")
        xg = cw_flat[:, 0:UE * TJ * D].rearrange("p (u j d) -> p u j d", j=TJ, d=D)
        xgT2 = sb("xgT2", [P, 2, DC, CAP])
        xgT = [xgT2[:, 0, :, :], xgT2[:, 1, :, :]] + [t[:, 0:DC * CAP].rearrange("p (k n) -> p k n", n=CAP) for t in (
            x_g[:, :, :].rearrange("p t d -> p (t d)"), xT_g[:, :, :].rearrange("p k n -> p (k n)"))]
        sg = sb("sg", [P, 2, CAP])
        hh = sb("hh", [P, 2, 2, CAP])
        yo = [t[:, b * TJ * D:(b + 1) * TJ * D].rearrange("p (j d) -> p j d", d=D)
              for t in (sil[:, :, :].rearrange("p c n -> p (c n)"), OH[:, :, :].rearrange("p k n -> p (k n)")) for b in range(2)]
        yin = [cw_flat[:, h * TT * D:(h + 1) * TT * D].rearrange("p (t d) -> p t d", d=D) for h in (1, 0)]
        assert UE * TJ * D <= TT * D

        bank = [ctx.enter_context(nc.psum_tensor(f"bank{i}", [P, 512], F32)) for i in range(8)]
        bankb = bank[1][:, :].bitcast(BF16)

        COND = [6, 7, 4, 5]
        NP = BG // 2
        GUB = [4, 0, 2]

        def gcol(b, k, lo, n):
            o = k * (FR + CU + FT + FR) + lo
            return wb[b][:, o:o + n]

        def g_first(b, k): return gcol(b, k, 0, FR)
        def rest(b, k): return gcol(b, k, FR, CU + FT)
        def u_first(b, k): return gcol(b, k, FR + CU + FT, FR)
        def down_first(b): return wb[b][:, WROW - D:WROW]

        s_tick = sem("tick")
        s_const = sem("consts_made")
        s_dve0 = sem("dve_setup")
        s_ids = sem("ids_loaded")
        s_wall = sem("mix_weights_loaded")
        s_w = sem("layer_weights_loaded")
        s_ws = sem("shared_weights_loaded")
        s_init = sem("scratch_initialised")
        s_x = sem("x_loaded")
        s_xT = sem("xT_loaded")
        s_pf = sem("pairs_free")
        s_mix = sem("mixed_in_psum")
        s_h0 = sem("h0_ready")
        s_hp = sem("hidden_in_psum")
        s_h = sem("hidden_ready")
        s_vx = sem("vx_in_psum")
        s_lp = sem("mixture_logits_in_psum")
        s_e = sem("mixture_exp_in")
        s_eo = sem("mixture_exp_out")
        s_al = sem("alpha_split")
        s_aTp = sem("alphaT_in_psum")
        s_aT = sem("alphaT_ready")
        s_sp = sem("spread_in_psum")
        s_spr = sem("spread_ready")
        s_z = sem("z_ready")
        s_up = sem("u_in_psum")
        s_x1 = sem("x1_ready")
        s_x1p = sem("x1_rows_in_psum")
        s_base = sem("base_ready")
        s_cw = sem("cond_weights_loaded")
        s_fs3 = sem("bias0_parts_made")
        s_bias0 = sem("bias0_ready")
        s_hz = sem("hidden_zeroed")
        s_cb3 = sem("bias_parts_made")
        s_cbk = sem("bias_parts_moved")
        s_cp = sem("cond_rows_in_psum")
        s_cta = sem("cond_rows_ready_scalar")
        s_ctv = sem("cond_rows_ready_vector")
        s_cTp = sem("condT_in_psum")
        s_cTa = sem("condT_ready_scalar")
        s_cTv = sem("condT_ready_vector")
        s_cv = sem("sums_chain")
        s_rows = sem("cond_rows_stored")
        s_rp = sem("router_logits_in_psum")
        s_m8 = sem("router_shifted")
        s_m8e = sem("router_exp_out")
        s_M = sem("choice_mask_ready")
        s_rk = sem("rank_in_psum")
        s_rkr = sem("rank_read")
        s_pair = sem("pairs_ready")
        s_scat = sem("pairs_scattered")
        s_v = sem("vector_chain")
        s_sh = sem("shared_in_psum")
        s_sil = sem("shared_silu_ready")
        s_hs = sem("shared_hidden_ready")
        s_sdp = sem("shared_down_in_psum")
        s_sb = sem("shared_added")
        s_cS = sem("former_groups_condT_loaded")
        s_cS3 = sem("last_groups_condT_moved")
        s_flags = sem("flags_ready")
        s_land = sem("rows_landed")
        s_fl = sem("flags_chain")
        s_lst = sem("slot_table_loaded")
        s_wb = [sem(f"expert_weights_loaded{i}") for i in range(UE)]
        s_gid = sem("gather_ids_copied")
        s_ids2 = sem("slot_ids_copied")
        s_xg = [sem(f"tokens_gathered{i}") for i in range(UE)]
        s_xp = sem("tokensT_in_psum")
        s_xs = sem("tokensT_ready_scalar")
        s_xv = sem("tokensT_ready_vector")
        s_gu = sem("gate_up_in_psum")
        s_sg = sem("silu_ready")
        s_hh = sem("expert_hidden_ready")
        s_dp = sem("down_in_psum")
        s_ys = sem("rows_ready_scalar")
        s_yv = sem("rows_ready_vector")
        s_acc = [sem(f"rows_added{j}") for j in range(2)]
        s_yin = [[sem(f"sums{j}_loaded{q}") for q in range(G)] for j in range(2)]
        s_fin = sem("output_ready")
        s_out = sem("output_stored")

        def by_tiles(eng, size, work):
            with eng.If(size > THREE):
                work(3)
            with eng.Else():
                with eng.If(size > TWO):
                    work(2)
                with eng.Else():
                    work(1)

        def notes(eng, shift=1):
            known = {}

            def get(what, e, u):
                if (what, u) not in known:
                    known[what, u] = eng.value_load(facts[0:1, what, bass.ds(e, 1)], min_val=0, max_val=16 * (TJ * E + TJ))
                return known[what, u]

            def start(e, u):
                if u == (LOOPS * UL + shift if isinstance(e, int) else shift):
                    known.clear()
            return get, start

        def all_steps(eng, step, shift=1):
            for e in range(shift):
                step(e, e, first=True)
            with eng.Fori(0, LOOPS) as i:
                for u in range(shift, UL + shift):
                    step(i * UL + u, u)
            for e in range(LOOPS * UL + shift, E):
                step(e, e)

        block = ctx.enter_context(nc.Block())
        PV = 28
        TAIL = 4

        @block.sync
        def _(sp):
            sp.dma_start(i_q0[:, :], idq0).then_inc(s_ids, 16)
            sp.dma_start(i_b0[:, :], idb0).then_inc(s_ids, 16)
            sp.dma_start(i_b1[:, :], idb1).then_inc(s_ids, 16)
            for q in range(BT):
                sp.dma_start(wall[q * S:(q + 1) * S], w0.rearrange("n c d -> c n d")).then_inc(s_wall, 16)
            sp.dma_start(fs_s[:, :], fs0).then_inc(s_wall, 16)
            sp.dma_start(x_g[:, :, :], x[0:GT, :].rearrange("(t p) d -> p t d", p=P)).then_inc(s_x, 16)
            sp.dma_start(W1s[:, :, :], W1.rearrange("(k p) n -> p k n", p=P)).then_inc(s_w, 16)
            sp.dma_start(b1s[:, :], b1).then_inc(s_w, 16)
            sp.dma_start(W2s[:, :, :], W2.rearrange("(k p) n -> p k n", p=P)).then_inc(s_w, 16)
            sp.dma_start(b2s[:, :], b2.rearrange("(a n) -> a n", a=1).to_broadcast([P, K0])).then_inc(s_w, 16)
            sp.dma_start(VTs[:, :, :], VT.rearrange("(k p) n -> p k n", p=P)).then_inc(s_w, 16)
            sp.dma_start(xT_g[:, :, :], xT[:, 0:GT].rearrange("(k p) n -> p k n", p=P)).then_inc(s_xT, 16)
            sp.dma_start(UTs[:, :, :], UT.rearrange("(k p) n -> p k n", p=P)).then_inc(s_w, 16)
            sp.dma_start(cbs[:, :], cb).then_inc(s_w, 16)
            sp.dma_start(gTs[:, :, :], gT.rearrange("(k p) n -> p k n", p=P)).then_inc(s_w, 16)

            for n in range(NS1):
                sp.dma_start(cw[:, n, :, :], cW[n].rearrange("(k p) n -> p k n", p=P)).then_inc(s_cw, 16)
            for a in range(3):
                sp.wait_ge(s_cb3, 2)
                sp.dma_start(cbk[a:a + 1, :, :], cb3[:, a, :]).then_inc(s_cbk, 16)
            sp.dma_start(sgus[:, :, :, :], sgu.rearrange("(k p) a n -> p k a n", p=P)).then_inc(s_ws, 16)
            for c, (lo, n) in enumerate(SCH):
                sp.dma_start(sds[0:n, c, :], sd[lo:lo + n, :]).then_inc(s_ws, 16)
            sp.wait_ge(s_const, 4)
            sp.dma_start(table.rearrange("(p n) c -> p (n c)", p=P), linit[:, :, :].rearrange("p n c -> p (n c)")).then_inc(s_init, 16)
            sp.dma_start(rows[N:NROWS, :].rearrange("(j p) d -> p j d", p=P), zrow[:, :].unsqueeze(1).to_broadcast([P, TJ, D])).then_inc(s_init, 16)

            def group(g, last):
                if not last:
                    sp.wait_ge(s_mix, 2 * g + 2)
                    sp.sem_inc(s_tick, 1)
                    sp.dma_start(x_g[:, :, :], x[bass.ds((g + 1) * GT, GT), :].rearrange("(t p) d -> p t d", p=P)).then_inc(s_x, 16)
                    sp.wait_ge(s_x1, 2 * g + 2)
                    sp.sem_inc(s_tick, 1)
                    sp.dma_start(xT_g[:, :, :], xT[:, bass.ds((g + 1) * GT, GT)].rearrange("(k p) n -> p k n", p=P)).then_inc(s_xT, 16)
                else:
                    sp.wait_ge(s_mix, 2 * G)
                    sp.wait_ge(s_rows, 48 * (G - 1))
                    sp.dma_start(cTs[:, 0:G - 1, :, :].rearrange("p g k n -> p g (k n)"), condT_rows.rearrange("g p n -> p g n")).then_inc(s_cS, 16)
                for h in range(2):
                    sp.wait_ge(s_cta, (2 * g + h + 1) * NP // 4)
                    sp.wait_ge(s_ctv, (2 * g + h + 1) * NP // 4)
                    sp.sem_inc(s_tick, 1)
                    sp.dma_start(rows[bass.ds((2 * g + h) * (GT // 2), GT // 2), :].rearrange("(b s) d -> s b d", s=S), ctok[h]).then_inc(s_rows, 16)
                sp.wait_ge(s_cTa, 2 * g + 2)
                sp.wait_ge(s_cTv, 2 * g + 2)
                sp.sem_inc(s_tick, 1)
                flat = cT[:, :, :].rearrange("p k n -> p (k n)")
                if last:
                    sp.dma_start(cTs[:, G - 1, :, :].rearrange("p k n -> p (k n)"), flat).then_inc(s_cS3, 16)
                else:
                    sp.dma_start(condT_rows[bass.ds(g, 1), :, :].rearrange("a p n -> p (a n)"), flat).then_inc(s_rows, 16)

            with sp.Fori(0, G - 1) as g:
                group(g, False)
            group(G - 1, True)

            def weights(e, b):
                sp.dma_start(wb[b], wblk[bass.ds(e, 1), :, :].rearrange("a p n -> p (a n)")).then_inc(s_wb[b], 16)
                sp.dma_start(wt[b], wdt[bass.ds(e, 1), :, :].rearrange("a p n -> p (a n)")).then_inc(s_wb[b], 16)

            weights(0, 0)
            weights(1, 1)
            sp.wait_ge(s_scat, 16 * TOPK * TT)
            sp.dma_start(lst[:, 0:E * TJ, :].rearrange("p n c -> p (n c)"), table.rearrange("(p n) c -> p (n c)", p=P)).then_inc(s_lst, 16)
            weights(2, 2)
            weights(3, 3)
            with sp.Fori(0, E // UE - 1) as i:
                for u in range(UE):
                    sp.wait_ge(s_dp, 2 * (UE * i + u + 1))
                    sp.sem_inc(s_tick, 1)
                    weights(UE * i + u + UE, u)
            for j in range(2):
                sp.wait_ge(s_land, E + 3 + j)
                for q in range(G):
                    sp.dma_start(yin[j][:, q * TG:(q + 1) * TG, :], acc[j][q * GT:(q + 1) * GT, :].rearrange("(t p) d -> p t d", p=P))\
                      .then_inc(s_yin[j][q], 16)
            for q in range(G):
                sp.wait_ge(s_fin, q + 1)
                sp.dma_start(out[q * GT:(q + 1) * GT, :].rearrange("(t p) d -> p t d", p=P), base[:, q * TG:(q + 1) * TG, :]).then_inc(s_out, 16)
            sp.wait_ge(s_out, 16 * G)

        @block.gpsimd
        def _(pool):
            pool.sem_inc(s_pf, 1)
            pool.sem_inc(s_land, 2)
            pool.memset(zrow[:, :], 0.0)
            pool.memset(linit[:, :, :], 0)
            pool.memset(ident[:, :], 0.0)
            pool.memset(tri[:, :], 1.0)
            pool.memset(sel[:, :], 1.0)
            pool.memset(onesb[:, :], 1.0)
            pool.iota(e_off_i[:, :], [[TJ, E]], base=0, channel_multiplier=0)
            pool.iota(iota_i[:, :], [[1, E]], base=0, channel_multiplier=0)
            pool.memset(onesf[:, :], 1.0)
            pool.iota(pcol_i[:, :], [[0, 1]], base=0, channel_multiplier=1)
            pool.iota(tokid[:, :], [[P, TT]], base=0, channel_multiplier=1).then_inc(s_const, 1)
            pool.wait_ge(s_const, 1)
            pool.affine_select(out=ident[:, :], in_=ident[:, :], compare_op=ALU.not_equal, fill=1.0, base=0,
                               pattern=[[-1, P]], channel_multiplier=1)
            pool.affine_select(out=tri[:, :], in_=tri[:, :], compare_op=ALU.is_gt, fill=0.0, base=0,
                               pattern=[[1, P]], channel_multiplier=-1).then_inc(s_const, 1)
            selv = sel[:, :].rearrange("p (k r) -> p k r", r=R0)
            pool.affine_select(out=selv, in_=selv, compare_op=ALU.is_ge, fill=0.0, base=0,
                               pattern=[[-3, K0], [0, R0]], channel_multiplier=1)
            pool.iota(linit[:, :, 0].rearrange("p (e j) -> p e j", j=TJ), [[0, E], [P, TJ]], base=N, channel_multiplier=1).then_inc(s_const, 1)
            pool.wait_ge(s_const, 3)
            pool.affine_select(out=selv, in_=selv, compare_op=ALU.is_ge, fill=0.0, base=2,
                               pattern=[[3, K0], [0, R0]], channel_multiplier=-1)
            pool.tensor_copy(identb[:, :], ident[:, :]).then_inc(s_const, 1)

            pool.wait_ge(s_fs3, 1)
            for lo, hi in ((0, BG), (BG, B)):
                for a in range(3):
                    last = pool.tensor_tensor(bias0[:, a, lo:hi, :], f_b0[:, lo:hi].unsqueeze(2).to_broadcast([NS0, hi - lo, S]),
                                              fs3[:, a, :].unsqueeze(1).to_broadcast([NS0, hi - lo, S]), ALU.mult)
                last.then_inc(s_bias0, 1)
            pool.memset(cbk[:, :, :], 0.0).then_inc(s_cb3, 1)
            pool.memset(hh[:, :, :, :], 0.0).then_inc(s_hz, 1)
            for j in range(2):
                pool.dma_start(acc[j].rearrange("(p r) d -> p r d", p=P),
                               zrow[:, :].unsqueeze(1).to_broadcast([P, NROWS // P, D])).then_inc(s_acc[j], 16)
            pool.wait_ge(s_init, 32)
            with pool.Fori(0, G) as g:
                pool.wait_ge(s_pair, g + 1)
                pool.sem_inc(s_tick, 1)
                for t in range(TG):
                    for k in range(TOPK):
                        pool.indirect_dma_start(table, bass.IndirectOffsetOnAxis(sli[:, k, t:t + 1], 0),
                                                pair[:, t, k, :], None, bounds_check=LROWS - 1, oob_is_err=False)\
                            .then_inc(s_scat, 16)
                pool.wait_ge(s_scat, (g + 1) * 16 * TOPK * TG)
                pool.sem_inc(s_pf, 1)

            def gathers(e, u):
                size = get(SIZE, e, u)
                pool.wait_ge(s_gid, e + 1)
                pool.sem_inc(s_tick, 1)

                def gather(j):
                    pool.indirect_dma_start(xg[:, u % UE, j, :], None, rows,
                                            bass.IndirectOffsetOnAxis(gids[:, u % UE, j:j + 1], 0)).then_inc(s_xg[u % UE], 16)

                gather(0)
                with pool.If(size > TWO):
                    gather(1)
                    with pool.If(size > THREE):
                        gather(2)

            def scatters(e, u):

                def scatter(j):
                    pool.indirect_dma_start(acc[u % 2], bass.IndirectOffsetOnAxis(sids[:, u % UE, j:j + 1], 0),
                                            yo[u % UE][:, j, :], None, compute_op=ALU.add).then_inc(s_acc[u % 2], 16)

                size, landed = get(SIZE, e, u), get(LANDED, e, u)
                pool.wait_ge(s_acc[u % 2], landed)
                pool.sem_inc(s_land, 1)
                pool.wait_ge(s_ys, 2 * e + 2)
                pool.sem_inc(s_tick, 1)
                scatter(0)
                pool.wait_ge(s_ys, 2 * e + 3)
                pool.wait_ge(s_yv, e + 2)
                pool.sem_inc(s_tick, 1)
                with pool.If(size > TWO):
                    scatter(1)
                    with pool.If(size > THREE):
                        scatter(2)

            pool.wait_ge(s_flags, 1)
            pool.wait_ge(s_lst, 16)
            pool.wait_ge(s_rows, 48 * G - 16)
            pool.sem_inc(s_tick, 1)
            get, start = notes(pool, 2)
            gathers(0, 0)
            gathers(1, 1)
            gathers(2, 2)
            gathers(3, 3)

            def step(e, u, first=False):
                start(e, u)
                if not (isinstance(e, int) and e >= E - 4):
                    pool.wait_ge(s_xp, 2 * e + 2)
                    pool.sem_inc(s_tick, 1)
                    gathers(e + 4, u + 4)
                if not first:
                    scatters(e - 2, u - 2)

            all_steps(pool, step, 2)
            scatters(E - 2, E - 2)
            scatters(E - 1, E - 1)
            landed = [pool.value_load(last_wait[0:1, j:j + 1], min_val=1, max_val=16 * (TJ * E + TJ)) for j in range(2)]
            for j in range(2):
                pool.wait_ge(s_acc[j], landed[j])
                pool.sem_inc(s_land, 1)

        @block.scalar
        def _(act):
            act.sem_inc(s_ys, 1)
            def hidden(g):
                act.wait_ge(s_mix, 2 * g + 1)
                act.activation(h0T[:, 0, :], bank[0][:, :], ACT.Copy).then_inc(s_h0, 1)
                for c in range(DC):
                    act.wait_ge(s_hp, 2 * g + 1 + c)
                    act.activation(hT[:, c, :], bank[2 + c][:, :], ACT.Relu, bias=b1s[:, c:c + 1]).then_inc(s_h, 1)

            def group(g, last):
                act.wait_ge(s_e, g + 1)
                act.activation(alp[:, :, :], lg[:, :, :], ACT.Exp).then_inc(s_eo, 1)
                act.wait_ge(s_aTp, g + 1)
                act.activation(alT[:, :], bankb[0:3 * K0, 0:GT], ACT.Copy).then_inc(s_aT, 1)
                for c in range(KC):
                    act.wait_ge(s_sp, KC * g + c + 1)
                    if c >= 2:
                        act.wait_ge(s_z, KC * g + c - 1)
                    act.activation(spread[:, c % 2, :], bank[2 + c % 2][:, :], ACT.Copy).then_inc(s_spr, 1)
                for h in range(2):
                    act.wait_ge(s_x1p, 2 * g + h + 1)
                    act.activation(base[:, bass.ds(g * TG + 2 * h, 2), :],
                                   bank[4 + h][:, :].rearrange("p (t d) -> p t d", d=D), ACT.Copy).then_inc(s_base, 1)
                for t in range(TG):
                    act.wait_ge(s_cp, NP * g + 2 * t + 1)
                    act.activation(ctok[t // 2][:, 4 * (t % 2):4 * (t % 2) + 2, :], bank[COND[2 * t % 4]][0:S, :].rearrange("p (b d) -> p b d", d=D), ACT.Copy)\
                       .then_inc(s_cta, 1)
                    if t % 2:
                        act.wait_ge(s_cTp, TG * g + t)
                        act.activation(cT[:, :, (t - 1) * P:t * P], bank[t - 1][:, 0:D].rearrange("p (k n) -> p k n", n=P), ACT.Copy)\
                           .then_inc(s_cTa, 1)
                act.wait_ge(s_m8, g + 1)
                act.activation(Lm[:, :, :], Lm[:, :, :], ACT.Exp).then_inc(s_m8e, 1)
                act.activation(v8m[:, :, :], v8m[:, :, :], ACT.Exp).then_inc(s_m8e, 1)
                if not last:
                    hidden(g + 1)
                    act.wait_ge(s_rows, 48 * g + 48)

            hidden(0)
            with act.Fori(0, G - 1) as g:
                group(g, False)
            group(G - 1, True)
            with act.Fori(0, G) as g:
                for c, (lo, n) in enumerate(SCH):
                    act.wait_ge(s_sh, len(SCH) * g + c + 1)
                    act.activation(sil[0:n, c, :], bank[GUB[c]][0:n, :], ACT.Silu).then_inc(s_sil, 1)

            def tokens(e, u):
                act.wait_ge(s_xp, 2 * e + 1)
                act.activation(xgT[u % UE][:, 0, :], bank[0][:, 0:CAP], ACT.Copy).then_inc(s_xs, 1)

            def step(e, u, first=False):
                act.wait_ge(s_gu, 3 * e + 1)
                act.activation(sg[:, 0, :], bank[2][:, 0:CAP], ACT.Silu).then_inc(s_sg, 1)
                act.wait_ge(s_gu, 3 * e + 2)
                act.activation(sg[0:FT, 1, :], bank[4][0:FT, 0:CAP], ACT.Silu).then_inc(s_sg, 1)
                if not first:
                    rows_out(e - 1, u - 1)
                if not (isinstance(e, int) and e >= E - 2):
                    tokens(e + 2, u + 2)

            def rows_out(e, u):
                act.wait_ge(s_ids2, 2 * e + 2)
                act.wait_ge(s_land, e + 1)
                for j in range(2):
                    act.wait_ge(s_dp, 2 * e + 1 + j)
                    act.activation(yo[u % UE][:, j, :], bank[5 + j][:, 0:D], ACT.Copy, scale=wcol[:, u % UE, j:j + 1]).then_inc(s_ys, 1)

            tokens(0, 0)
            tokens(1, 1)
            all_steps(act, step)
            rows_out(E - 1, E - 1)

        @block.vector
        def _(dve):
            v = nc.vector
            done = [0, 0]

            def link(ins, g=0):
                done[1] += 1
                ins.then_inc(s_v, 1)
                before = done[0] - (0 if isinstance(g, int) and g == 0 else TAIL)
                dve.wait_ge(s_v, g * PV + (before + done[1]))

            def mixed(g):
                dve.wait_ge(s_mix, 2 * g + 2)
                v.tensor_copy(h0T[:, 1, :], bank[1][:, :]).then_inc(s_h0, 1)

            dve.sem_inc(s_yv, 1)
            dve.sem_inc(s_rkr, 1)
            v.memset(mc[:, :, :], 0.0)
            v.memset(gath0[:, :, :], 0.0)
            v.memset(bd, 0.0)
            dve.wait_ge(s_const, 1)
            v.tensor_copy(iota64[:, :], iota_i[:, :])
            v.tensor_copy(e_off[:, :], e_off_i[:, :])
            link(v.tensor_copy(pcol[:, :], pcol_i[:, :]))
            dve.wait_ge(s_ids, 48)
            v.tensor_copy(f_q0[:, :], i_q0[:, :])
            link(v.tensor_copy(f_b0[:, :], i_b0[:, :]))
            link(v.tensor_scalar(f_b0[:, :], f_b0[:, :], pcol[0:NS0, 0:1], None, ALU.is_equal))
            dve.wait_ge(s_wall, 16 * (BT + 1))
            link(v.tensor_copy(fs3[:, 0, :], fs_s[:, :]))
            link(v.tensor_tensor(fsr[:, :], fs_s[:, :], fs3[:, 0, :], ALU.subtract))
            link(v.tensor_copy(fs3[:, 1, :], fsr[:, :]))
            link(v.tensor_tensor(fsr[:, :], fsr[:, :], fs3[:, 1, :], ALU.subtract))
            v.tensor_copy(fs3[:, 2, :], fsr[:, :]).then_inc(s_fs3, 1)
            for n in range(NS0):
                last = v.tensor_scalar(maskq[:, n, :], f_q0[:, :], float(n), None, ALU.is_equal)
            link(last)
            for lo, hi in ((0, TG), (TG, TT)):
                for n in range(NS0):
                    link(v.copy_predicated(gath0[:, lo:hi, :], maskq[:, n, lo:hi].unsqueeze(2).to_broadcast([P, hi - lo, S]),
                                           wall[:, n, :].unsqueeze(1).to_broadcast([P, hi - lo, S])))
                for q in range(BT):
                    last = v.tensor_copy(bd[q * S:(q + 1) * S, lo:hi, q * S:(q + 1) * S], gath0[q * S:(q + 1) * S, lo:hi, :])
                last.then_inc(s_dve0, 1)
            mixed(0)
            dve.wait_ge(s_w, 16 * 8)
            link(v.tensor_copy(cb3[:, 0, :], cbs[:, :]))
            link(v.tensor_tensor(cbr[:, :], cbs[:, :], cb3[:, 0, :], ALU.subtract))
            link(v.tensor_copy(cb3[:, 1, :], cbr[:, :]))
            link(v.tensor_tensor(cbr[:, :], cbr[:, :], cb3[:, 1, :], ALU.subtract))
            v.tensor_copy(cb3[:, 2, :], cbr[:, :]).then_inc(s_cb3, 1)
            done[0], done[1] = done[1], 0

            def shared_hidden(g, c):
                n = SCH[c][1]
                dve.wait_ge(s_sil, len(SCH) * g + c + 1)
                v.tensor_tensor(hs[0:n, c, :], sil[0:n, c, :], bank[GUB[c] + 1][0:n, :], ALU.mult).then_inc(s_hs, 1)

            def shared_add(g):
                for h in range(2):
                    dve.wait_ge(s_sdp, 2 * g + h + 1)
                    rows2 = base[:, bass.ds(g * TG + 2 * h, 2), :]
                    v.tensor_tensor(rows2, rows2, bank[7 - h][:, :].rearrange("p (t d) -> p t d", d=D), ALU.add).then_inc(s_sb, 1)

            def slots_of_choices(g):
                link(v.tensor_tensor(sa[:, :], sa[:, :], sbb[:, :], ALU.add), g)
                link(v.tensor_tensor(sc[:, :], sc[:, :], sa[:, :], ALU.add), g)
                link(v.tensor_tensor(OH[:, :, :], OH[:, :, :], sc[:, :].unsqueeze(1).to_broadcast([P, TOPK, TG * E]), ALU.mult), g)
                link(v.reduce_sum(slf[:, :, :], OH[:, :, :].rearrange("p k (t e) -> p k t e", e=E), AX.X), g)
                v.tensor_copy(sli[:, :, :], slf[:, :, :]).then_inc(s_pair, 1)

            def group(g, last_group, first=False):
                done[1] = 0
                dve.wait_ge(s_lp, g + 1)
                link(v.tensor_tensor(lg[:, :, :], bank[0][:, 0:TG * K0].rearrange("p (t k) -> p t k", k=K0),
                                     b2s[:, :].unsqueeze(1).to_broadcast([P, TG, K0]), ALU.add), g)
                link(v.reduce_max(lgm[:, :], lg[:, :, :], AX.X), g)
                v.tensor_tensor(lg[:, :, :], lg[:, :, :], lgm[:, :].unsqueeze(2).to_broadcast([P, TG, K0]),
                                ALU.subtract).then_inc(s_e, 1)
                dve.wait_ge(s_eo, g + 1)
                link(v.reduce_sum(lgm[:, :], alp[:, :, :], AX.X), g)
                link(v.reciprocal(lgm[:, :], lgm[:, :]), g)
                link(v.tensor_tensor(alp[:, :, :], alp[:, :, :], lgm[:, :].unsqueeze(2).to_broadcast([P, TG, K0]), ALU.mult), g)
                link(v.tensor_copy(als[:, :, :, 0], alp[:, :, :]), g)
                link(v.tensor_tensor(alr[:, :, :], alp[:, :, :], als[:, :, :, 0], ALU.subtract), g)
                link(v.tensor_copy(als[:, :, :, 1], alr[:, :, :]), g)
                link(v.tensor_tensor(alr[:, :, :], alr[:, :, :], als[:, :, :, 1], ALU.subtract), g)
                v.tensor_copy(als[:, :, :, 2], alr[:, :, :]).then_inc(s_al, 1)
                for c in range(KC):
                    dve.wait_ge(s_vx, KC * g + c + 1)
                    dve.wait_ge(s_spr, KC * g + c + 1)
                    v.tensor_tensor(z[:, c, :], spread[:, c % 2, :], bank[4 + c][:, :], ALU.mult).then_inc(s_z, 1)
                dve.wait_ge(s_xT, 16 * g + 16)
                for c in range(DC):
                    dve.wait_ge(s_up, DC * g + c + 1)
                    v.tensor_tensor(x1T[:, c, :], xT_g[:, c, :], bank[c][:, :], ALU.add).then_inc(s_x1, 1)
                if not first:
                    slots_of_choices(g)
                for t in range(TG):
                    dve.wait_ge(s_cp, NP * g + 2 * t + 2)
                    v.tensor_copy(ctok[t // 2][:, 4 * (t % 2) + 2:4 * (t % 2) + 4, :], bank[COND[(2 * t + 1) % 4]][0:S, :].rearrange("p (b d) -> p b d", d=D))\
                        .then_inc(s_ctv, 1)
                    if t >= 2:
                        h = t - 2
                        dve.wait_ge(s_cTp, TG * g + 2 * h + 2)
                        v.tensor_copy(cT[:, :, (2 * h + 1) * P:(2 * h + 2) * P], bank[2 * h + 1][:, 0:D].rearrange("p (k n) -> p k n", n=P)).then_inc(s_cTv, 1)
                dve.wait_ge(s_rp, g + 1)
                link(v.tensor_copy(Ls[:, :, :].rearrange("p t e -> p (t e)"), bank[6][:, 0:TG * E]), g)
                dve.sem_inc(s_tick, 1)
                for t in range(TG):
                    last = v.max(v8[:, t, :], Ls[:, t, :])
                link(last, g)
                v.tensor_tensor(Lm[:, :, :], Ls[:, :, :], v8[:, :, 0:1].to_broadcast([P, TG, E]), ALU.subtract)
                v.tensor_tensor(v8m[:, :, :], v8[:, :, :], v8[:, :, 0:1].to_broadcast([P, TG, 8]), ALU.subtract).then_inc(s_m8, 1)
                for t in range(TG):
                    last = v.max_index(i8[:, t, :], v8[:, t, :], Ls[:, t, :])
                link(last, g)
                v.tensor_copy(mc[:, 0, :], mc[:, TG, :])
                link(v.tensor_copy(i8f[:, :, :], i8[:, :, :]), g)
                if not last_group:
                    mixed(g + 1)
                for k in range(TOPK):
                    last = v.tensor_tensor(OH[:, k, :].rearrange("p (t e) -> p t e", e=E),
                                           iota64[:, :].unsqueeze(1).to_broadcast([P, TG, E]),
                                           i8f[:, :, k:k + 1].to_broadcast([P, TG, E]), ALU.is_equal)
                link(last, g)
                with nc.allow_low_precision(reason="counts up to 16 are exact"):
                    link(v.reduce_sum(M[:, :], OH[:, :, :].rearrange("p k n -> p n k"), AX.X), g)
                    for t in range(TG):
                        last = v.tensor_tensor(mc[:, t + 1, :], mc[:, t, :], M[:, t * E:(t + 1) * E], ALU.add)
                        if t < TG - 1:
                            link(last, g)
                last.then_inc(s_M, 1)

                if last_group:
                    shared_hidden(0, 0)
                    shared_hidden(0, 1)
                dve.wait_ge(s_m8e, 2 * g + 2)
                link(v.reduce_sum(zs[:, :], Lm[:, :, :], AX.X), g)
                link(v.reciprocal(zs[:, :], zs[:, :]), g)
                link(v.tensor_tensor(v8m[:, :, :], v8m[:, :, :], zs[:, :].unsqueeze(2).to_broadcast([P, TG, 8]), ALU.mult), g)
                link(v.reduce_sum(s6[:, :], v8m[:, :, 0:TOPK], AX.X), g)
                link(v.tensor_scalar(s6[:, :], s6[:, :], 1e-20, None, ALU.add), g)
                link(v.reciprocal(s6[:, :], s6[:, :]), g)
                dve.wait_ge(s_pf, g + 1)
                v.tensor_tensor(pair[:, :, :, 1].bitcast(F32), v8m[:, :, 0:TOPK],
                                s6[:, :].unsqueeze(2).to_broadcast([P, TG, TOPK]), ALU.mult)
                v.tensor_copy(pair[:, :, :, 0], tokid[:, bass.ds(g * TG, TG)].unsqueeze(2).to_broadcast([P, TG, TOPK]))
                if last_group:
                    shared_hidden(0, 2)
                dve.wait_ge(s_rk, g + 1)
                v.tensor_scalar(sa[:, :], bank[6][:, TG * E:2 * TG * E], float(P), float(1 - LROWS), ALU.is_ge, ALU.mult)
                v.tensor_scalar(sbb[:, :], bank[6][:, TG * E:2 * TG * E], float(2 * P), float(1 - LROWS), ALU.is_ge, ALU.mult)
                v.scalar_tensor_tensor(sc[:, :].rearrange("p (t e) -> p t e", e=E), bank[6][:, TG * E:2 * TG * E].rearrange("p (t e) -> p t e", e=E),
                                       float(E * TJ), e_off[:, :].unsqueeze(1).to_broadcast([P, TG, E]), ALU.mult, ALU.add).then_inc(s_rkr, 1)
                if last_group:
                    for i, n in enumerate(SIZES[:-1]):
                        last = v.tensor_scalar(more[:, i, :], bank[6][:, 0:E], n + 0.5, None, ALU.is_ge)
                    last.then_inc(s_fl, 1)
                dve.wait_ge(s_rkr, g + 2)
                if last_group:
                    slots_of_choices(g)
                if not last_group:
                    dve.wait_ge(s_rows, 48 * g + 48)
                assert done[1] == PV - TAIL * first + TAIL * last_group, done

            group(0, False, first=True)
            with dve.Fori(1, G - 1) as g:
                group(g, False)
            group(G - 1, True)

            steps = [0]

            def flink(ins):
                steps[0] += 1
                ins.then_inc(s_fl, 1)
                dve.wait_ge(s_fl, steps[0])

            steps[0] = 1
            dve.wait_ge(s_fl, 1)
            with nc.allow_low_precision(reason="counts up to 4 are exact"):
                v.reduce_sum(facts[:, SIZE, :], more[:, :, :].rearrange("p i e -> p e i"), AX.X)
            flink(v.tensor_tensor(tiles_f[:, :], more[:, SIZES.index(P), :], more[:, SIZES.index(2 * P), :], ALU.add))
            flink(v.tensor_scalar(tiles_f[:, :], tiles_f[:, :], 1.0, None, ALU.add))
            for u in range(2):
                last = v.tensor_tensor_scan(seen[:, u:E:2], onesf[:, 0:E:2], tiles_f[:, u:E:2], 0.0, ALU.mult, ALU.add)
            flink(last)
            flink(v.tensor_tensor(fl[:, :], seen[:, :], tiles_f[:, :], ALU.subtract))
            v.tensor_scalar(facts[:, LANDED, :], fl[:, :], 16.0, 16.0, ALU.mult, ALU.add)
            flink(v.tensor_scalar(last_wait[:, :], seen[:, E - 2:E], 16.0, 16.0, ALU.mult, ALU.add))
            for u in range(UE):
                last = v.tensor_tensor_scan(seen[:, u:E:UE], onesf[:, 0:E:UE], tiles_f[:, u:E:UE], 0.0, ALU.mult, ALU.add)
            flink(last)
            v.tensor_scalar(facts[:, GATHERED, :], seen[:, :], 16.0, None, ALU.mult).then_inc(s_flags, 1)

            dve.wait_ge(s_base, 2 * G)
            shared_add(0)

            def shared(g):
                for c in range(len(SCH)):
                    shared_hidden(g, c)
                shared_add(g)

            def gather_ids(e, u):
                v.tensor_copy(gids[:, u % UE, :], lst[:, bass.ds(e * TJ, TJ), 0]).then_inc(s_gid, 1)

            with dve.Fori(1, G - 1) as g:
                shared(g)
            dve.wait_ge(s_lst, 16)
            for e in range(4):
                gather_ids(e, e)
            shared(G - 1)

            def tokens(e, u):
                dve.wait_ge(s_xp, 2 * e + 2)
                v.tensor_copy(xgT[u % UE][:, 1, :], bank[1][:, 0:CAP]).then_inc(s_xv, 1)

            def slots(e, u):
                dve.wait_ge(s_land, e + 1)
                dve.sem_inc(s_tick, 1)
                v.tensor_copy(sids[:, u % UE, :], lst[:, bass.ds(e * TJ, TJ), 0]).then_inc(s_ids2, 1)
                v.tensor_copy(wcol[:, u % UE, :], lst[:, bass.ds(e * TJ, TJ), 1].bitcast(F32)).then_inc(s_ids2, 1)

            def rows_out(e, u):
                dve.wait_ge(s_ids2, 2 * e + 2)
                dve.wait_ge(s_land, e + 1)
                dve.wait_ge(s_dp, 2 * e + 2)
                v.tensor_scalar(yo[u % UE][:, 2, :], bank[7][:, 0:D], wcol[:, u % UE, 2:3], None, ALU.mult).then_inc(s_yv, 1)

            def step(e, u, first=False):
                dve.wait_ge(s_gu, 3 * e + 2)
                dve.wait_ge(s_sg, 2 * e + 2)
                v.tensor_tensor(hh[0:FT, u % 2, 1, :], sg[0:FT, 1, :], bank[4][CU:CU + FT, 0:CAP], ALU.mult).then_inc(s_hh, 1)
                dve.wait_ge(s_gu, 3 * e + 3)
                v.tensor_tensor(hh[:, u % 2, 0, :], sg[:, 0, :], bank[3][:, 0:CAP], ALU.mult).then_inc(s_hh, 1)
                if not first:
                    rows_out(e - 1, u - 1)
                if not (isinstance(e, int) and e >= E - 2):
                    tokens(e + 2, u + 2)
                slots(e, u)
                if not (isinstance(e, int) and e >= E - 5):
                    gather_ids(e + 5, u + 5)

            dve.wait_ge(s_hz, 1)
            tokens(0, 0)
            gather_ids(4, 4)
            tokens(1, 1)
            all_steps(dve, step)
            rows_out(E - 1, E - 1)

            for j in range(2):
                for q in range(G):
                    dve.wait_ge(s_yin[j][q], 16)
                    if j:
                        dve.wait_ge(s_cv, q + 1)
                    part = base[:, q * TG:(q + 1) * TG, :]
                    v.tensor_tensor(part, part, yin[j][:, q * TG:(q + 1) * TG, :], ALU.add).then_inc(s_fin if j else s_cv, 1)

        @block.tensor
        def _(pe):
            mm, tr = nc.tensor.matmul, nc.tensor.transpose
            pe.wait_ge(s_dve0, 1)
            pe.wait_ge(s_bias0, 1)
            pe.wait_ge(s_const, 4)
            def vx(o):
                for c in range(DC):
                    last = mm(bank[4 + o][:, :], VTs[:, c, o * P:(o + 1) * P], h0T[:, c, :], start=c == 0, stop=c == DC - 1)
                last.then_inc(s_vx, 1)

            def mix(g):
                pe.wait_ge(s_x, 16 * g + 16)
                for c in range(DC):
                    for a in range(3):
                        mm(bank[c][:, :], onesb[0:NS0, :], bias0[:, a, bass.ds(g * BG, BG), :].rearrange("p b s -> p (b s)"),
                           start=a == 0, stop=False)
                    for t in range(TG):
                        o = bank[c][:, t * P:(t + 1) * P]
                        last = mm(o, x_g[:, t, c * P:(c + 1) * P], bd[:, bass.ds(g * TG + t, 1), :].rearrange("p a n -> p (a n)"),
                           start=False, stop=t == TG - 1)
                    last.then_inc(s_mix, 1)
                pe.wait_ge(s_w, 16 * 8)
                pe.wait_ge(s_h0, 2 * g + 2)
                for o in range(DC):
                    for c in range(DC):
                        last = mm(bank[2 + o][:, :], W1s[:, c, o * P:(o + 1) * P], h0T[:, c, :], start=c == 0, stop=c == DC - 1)
                    last.then_inc(s_hp, 1)
                vx(0)

            def group(g, last_group):
                pe.wait_ge(s_h, 2 * g + 2)
                for t in range(TG):
                    for c in range(DC):
                        last = mm(bank[0][:, t * K0:(t + 1) * K0], hT[:, c, t * P:(t + 1) * P], W2s[:, c, :],
                                  start=c == 0, stop=c == DC - 1)
                last.then_inc(s_lp, 1)
                for o in range(1, KC - 1):
                    if o == 2:
                        pe.wait_ge(s_rkr, g + 1)
                    vx(o)
                pe.wait_ge(s_al, g + 1)
                for t in range(TG):
                    last = tr(bankb[0:3 * K0, t * P:(t + 1) * P], als[:, t, :, :].rearrange("p k a -> p (k a)"), identb[:, :])
                last.then_inc(s_aTp, 1)
                vx(KC - 1)
                pe.wait_ge(s_aT, g + 1)

                def spread_alpha(c):
                    if c >= 2:
                        pe.wait_ge(s_spr, KC * g + c - 1)
                    mm(bank[2 + c % 2][:, :], sel[:, c * P:(c + 1) * P], alT[:, :], start=True, stop=True).then_inc(s_sp, 1)

                for c in range(3):
                    spread_alpha(c)
                for c in range(KC):
                    pe.wait_ge(s_z, KC * g + c + 1)
                    for o in range(DC):
                        last = mm(bank[o][:, :], UTs[:, c, o * P:(o + 1) * P], z[:, c, :], start=c == 0, stop=c == KC - 1)
                        if c == KC - 1:
                            last.then_inc(s_up, 1)
                    if c == 0:
                        for c2 in range(3, KC):
                            spread_alpha(c2)
                for c in range(DC):
                    pe.wait_ge(s_x1, 2 * g + c + 1)
                    for t in range(TG):
                        last = tr(bank[4 + t // 2][:, (t % 2) * D + c * P:(t % 2) * D + (c + 1) * P], x1T[:, c, t * P:(t + 1) * P], ident[:, :])
                        if t % 2 and c == DC - 1:
                            last.then_inc(s_x1p, 1)

                def cond(p):
                    for m in (2 * p, 2 * p + 1):
                        o = bank[COND[p % 4]][0:S, (m % 2) * D:(m % 2 + 1) * D]
                        which = pe.value_load(i_b1[0:1, bass.ds(g * BG + m, 1)], min_val=0, max_val=NS1 - 1)
                        mm(o, onesb[:, 0:S], cbk[:, bass.ds(which, 1), :].rearrange("p a n -> p (a n)"), start=True, stop=False)
                        for c in range(DC):
                            last = mm(o, x1T[:, c, m * S:(m + 1) * S], cw[:, bass.ds(which, 1), c, :].rearrange("p a n -> p (a n)"),
                                      start=False, stop=c == DC - 1)
                    last.then_inc(s_cp, 1)

                def condT(t):
                    pe.wait_ge(s_cta, TG * g + t + 1)
                    pe.wait_ge(s_ctv, TG * g + t + 1)
                    pe.sem_inc(s_tick, 1)
                    for c in range(DC):
                        for q in range(BT):
                            last = tr(bank[t][:, c * P + q * S:c * P + (q + 1) * S], ctok[t // 2][:, 4 * (t % 2) + q, c * P:(c + 1) * P], ident[0:S, 0:S])
                    last.then_inc(s_cTp, 1)

                def router(t):
                    pe.wait_ge(s_cTv if t % 2 else s_cTa, 2 * g + t // 2 + 1)
                    for c in range(DC):
                        last = mm(bank[6][:, t * E:(t + 1) * E], cT[:, c, t * P:(t + 1) * P], gTs[:, c, :], start=c == 0, stop=c == DC - 1)
                    if t == TG - 1:
                        last.then_inc(s_rp, 1)

                pe.wait_ge(s_cw, 16 * NS1)
                pe.wait_ge(s_cbk, 48)
                cond(0)
                cond(1)
                pe.wait_ge(s_base, 2 * g + 2)
                cond(2)
                cond(3)
                condT(0)
                cond(4)
                cond(5)
                condT(1)
                cond(6)
                cond(7)
                condT(2)
                router(0)
                router(1)
                condT(3)
                router(2)
                router(3)
                if not last_group:
                    pe.wait_ge(s_bias0, 2)
                    pe.wait_ge(s_dve0, 2)
                    mix(g + 1)
                else:
                    shared_chunk(0, 0)
                    shared_chunk(0, 1)
                pe.wait_ge(s_M, g + 1)
                o = TG * E
                for t in range(TG):
                    mm(bank[6][:, o + t * E:o + (t + 1) * E], tri[:, :], M[:, t * E:(t + 1) * E], start=True, stop=False)
                    last = mm(bank[6][:, o + t * E:o + (t + 1) * E], onesb[:, :], mc[:, t, :], start=False, stop=True)
                if last_group:
                    last = mm(bank[6][:, 0:E], onesb[:, :], mc[:, TG, :], start=True, stop=True)
                last.then_inc(s_rk, 1)

            def shared_chunk(g, s_):
                lo, n = SCH[s_]
                if isinstance(g, int) and g == 0:
                    if s_ == 0:
                        pe.wait_ge(s_ws, 16 * (1 + len(SCH)))
                        pe.wait_ge(s_cS, 16)
                else:
                    pe.wait_ge(s_hs, len(SCH) * (g - 1) + s_ + 1)
                for a in range(2):
                    for c in range(DC):
                        last = mm(bank[GUB[s_] + a][0:n, :], sgus[:, c, a, lo:lo + n], cTs[:, bass.ds(g, 1), c, :].rearrange("p a n -> p (a n)"),
                                  start=c == 0, stop=c == DC - 1)
                last.then_inc(s_sh, 1)

            def shared_down(g):
                pe.wait_ge(s_hs, len(SCH) * (g + 1))
                for t in range(TG):
                    if t % 2 == 0 and not (isinstance(g, int) and g == 0):
                        pe.wait_ge(s_sb, 2 * (g - 1) + t // 2 + 1)
                    if t == 2 and isinstance(g, int) and g == 0:
                        pe.wait_ge(s_fl, 1)
                    for s_, (lo, n) in enumerate(SCH):
                        last = mm(bank[7 - t // 2][:, (t % 2) * D:(t % 2 + 1) * D], hs[0:n, s_, t * P:(t + 1) * P], sds[0:n, s_, :],
                                  start=s_ == 0, stop=s_ == len(SCH) - 1)
                    if t % 2:
                        last.then_inc(s_sdp, 1)

            mix(0)
            with pe.Fori(0, G - 1) as g:
                group(g, False)
            group(G - 1, True)
            shared_chunk(0, 2)
            shared_chunk(1, 0)
            shared_down(0)
            pe.wait_ge(s_cS3, 16)
            with pe.Fori(1, G - 1) as g:
                shared_chunk(g, 1)
                shared_chunk(g, 2)
                shared_chunk(g + 1, 0)
                shared_down(g)
            shared_chunk(G - 1, 1)
            shared_chunk(G - 1, 2)
            shared_down(G - 1)

            get, start = notes(pe)

            def tokens(e, u):
                def work(tiles):
                    pe.wait_ge(s_xg[u % UE], gathered)
                    if u:
                        pe.wait_ge(s_xs, e)
                        pe.wait_ge(s_xv, e)
                    for c in range(DC):
                        for j in range(tiles):
                            last = tr(bank[c][:, j * P:(j + 1) * P], xg[:, u % UE, j, c * P:(c + 1) * P], ident[:, :])
                        last.then_inc(s_xp, 1)

                gathered = get(GATHERED, e, u)
                by_tiles(pe, get(SIZE, e, u), work)

            def step(e, u, first=False):
                b = u % UE

                def gate_up(n):
                    pe.wait_ge(s_wb[b], (32 // UE) * (e - b + UE))
                    if isinstance(e, int) and e == E - 1:
                        pe.wait_ge(s_xs, e + 1)
                        pe.wait_ge(s_xv, e + 1)
                    if not first:
                        pe.wait_ge(s_hh, 2 * e)
                    for o, w, m in ((2, g_first, FR), (4, rest, CU + FT), (3, u_first, FR)):
                        for c in range(DC):
                            ins = mm(bank[o][0:m, 0:n], w(b, c), xgT[u % UE][:, c, 0:n], start=c == 0, stop=c == DC - 1)
                        ins.then_inc(s_gu, 1)

                start(e, u)
                by_rows(get(SIZE, e, u), gate_up)
                if not first:
                    down(e - 1, u - 1)
                if not (isinstance(e, int) and e >= E - 2):
                    tokens(e + 2, u + 2)

            def down(e, u):
                def work(tiles):
                    if u == E - 1:
                        pe.wait_ge(s_hh, 2 * e + 2)
                    pe.wait_ge(s_ys, 2 * e + 1)
                    pe.wait_ge(s_yv, e + 1)
                    for j in (0, 2, 1)[:1 if tiles == 1 else 3]:
                        if j < tiles:
                            o = bank[5 + j][:, 0:D]
                            mm(o, hh[:, u % 2, 0, j * P:(j + 1) * P], down_first(u % UE), start=True, stop=False)
                            last = mm(o, hh[0:FT, u % 2, 1, j * P:(j + 1) * P], wt[u % UE], start=False, stop=True)
                        if j != 2:
                            last.then_inc(s_dp, 2 if tiles == 1 else 1)

                by_tiles(pe, get(SIZE, e, u), work)

            def by_rows(size, work, lo=0, hi=len(SIZES)):
                if hi - lo == 1:
                    work(SIZES[lo])
                    return
                mid = (lo + hi) // 2
                with pe.If(size > mid - 1):
                    by_rows(size, work, mid, hi)
                with pe.Else():
                    by_rows(size, work, lo, mid)

            pe.wait_ge(s_flags, 1)
            pe.sem_inc(s_tick, 1)
            tokens(0, 0)
            tokens(1, 1)
            pe.wait_ge(s_sb, 2 * G)
            all_steps(pe, step)
            down(E - 1, E - 1)


IN = ["x", "xT", "idq0", "idb0", "idb1", "w0", "fs0", "W1", "b1", "W2", "b2", "VT", "UT", "cW", "cb", "gT", "wblk", "wdt", "sgu", "sd"]


def kernel(x, itok_B_0_7, fside_8xS_0, itok_B_0_15, L0_cond_weights, L0_ffn_U, L0_ffn_V, L0_ffn_W1, L0_ffn_b1,
           L0_ffn_W2, L0_ffn_b2, L1_cond_W, L1_cond_b, L1_ffn_gate_w, L1_ffn_w_gate, L1_ffn_w_up, L1_ffn_w_down,
           L1_ffn_sh_gate, L1_ffn_sh_up, L1_ffn_sh_down):
    import numpy as np
    import concourse.bacc as bacc
    from concourse.bass_utils import run_bass_kernel_spmd

    x2 = np.asarray(x).reshape(N, D)
    ids0, ids1 = np.asarray(itok_B_0_7), np.asarray(itok_B_0_15)

    def packed(w_gate, w_up, w_down):
        g = np.asarray(w_gate).transpose(0, 2, 1).reshape(E, DC, P, F).transpose(0, 2, 1, 3)
        u = np.asarray(w_up).transpose(0, 2, 1).reshape(E, DC, P, F).transpose(0, 2, 1, 3)
        gap = np.zeros((E, P, DC, CU - FT), g.dtype)
        gu = np.concatenate([g, gap, u[..., FR:], u[..., :FR]], axis=3).reshape(E, P, WROW - D)
        d = np.asarray(w_down).transpose(0, 2, 1)
        return np.concatenate([gu, d[:, :FR]], axis=2), d[:, FR:]

    wblk, wdt = packed(L1_ffn_w_gate, L1_ffn_w_up, L1_ffn_w_down)
    arrays = {
        "x": x2, "xT": x2.T,
        "idq0": np.repeat(ids0.reshape(TT, BT).T, S, axis=0),
        "idb0": np.repeat(ids0.reshape(1, B), NS0, axis=0),
        "idb1": ids1.reshape(1, B),
        "w0": L0_cond_weights, "fs0": fside_8xS_0,
        "W1": L0_ffn_W1, "b1": np.asarray(L0_ffn_b1).reshape(DC, P).T, "W2": L0_ffn_W2, "b2": L0_ffn_b2,
        "VT": np.asarray(L0_ffn_V).reshape(KR, D).T,
        "UT": np.asarray(L0_ffn_U).transpose(0, 2, 1).reshape(KR, D),
        "cW": L1_cond_W, "cb": L1_cond_b, "gT": np.asarray(L1_ffn_gate_w).T,
        "wblk": wblk, "wdt": wdt,
        "sgu": np.stack([np.asarray(L1_ffn_sh_gate).T, np.asarray(L1_ffn_sh_up).T], axis=1),
        "sd": np.asarray(L1_ffn_sh_down).T,
    }
    nc = bacc.Bacc("TRN2", target_bir_lowering=False, num_devices=1)
    aps = []
    for name in IN:
        a = np.ascontiguousarray(arrays[name])
        arrays[name] = a
        aps.append(nc.dram_tensor(f"in_{name}", a.shape, mybir.dt.from_np(a.dtype), kind="ExternalInput").ap())
    out = nc.dram_tensor("out_y", (N, D), F32, kind="ExternalOutput").ap()
    program(nc, *aps, out)
    r = run_bass_kernel_spmd(nc, [{f"in_{k}": a for k, a in arrays.items()}], core_ids=[0])
    return r.results[0]["out_y"].reshape(B, S, D)
```
